# Optimizing a Trainium2 kernel written in Bass

```python
import numpy as np
import jax
import jax.numpy as jnp

def _softmax(x, axis=-1):
    return jax.nn.softmax(x, axis=axis)

def _gelu(x):
    return jax.nn.gelu(x, approximate=True)

def _silu(x):
    return jax.nn.silu(x)

def _sigmoid(x):
    return jax.nn.sigmoid(x)

def _layernorm(x, axis=-1, eps=1e-05):
    m = jnp.mean(x, axis=axis, keepdims=True)
    v = jnp.var(x, axis=axis, keepdims=True)
    return (x - m) / jnp.sqrt(v + eps)

def _scatter_add(tgt, idx, src, axis=0):
    return tgt.at[idx].add(src)

def _segment_sum(src, seg, n):
    return jax.ops.segment_sum(src, seg, n)
kernel_name = 'mk_seq_postln_d1_jaxref_r8_803af0'

def setup_inputs(seed: int=0):
    np.random.seed(seed)
    _w = jnp.asarray

    def _L0_attn_setup():
        import jax, jax.numpy as jnp
        import numpy as np
        NUM_HEADS = 16
        HIDDEN = 128
        HEAD_DIM = HIDDEN // NUM_HEADS

        def _rope_cos_sin(S, head_dim):
            inv = 1.0 / 10000.0 ** (jnp.arange(0, head_dim, 2, dtype=jnp.float32) / head_dim)
            t = jnp.arange(S, dtype=jnp.float32)
            ang = jnp.outer(t, inv)
            return (jnp.cos(ang), jnp.sin(ang))

        def _apply_rope(x, cos, sin):
            B, S, nh, hd = x.shape
            xr = x[..., 0::2]
            xi = x[..., 1::2]
            c = cos[None, :, None, :]
            s = sin[None, :, None, :]
            or_ = xr * c - xi * s
            oi_ = xr * s + xi * c
            return jnp.stack([or_, oi_], axis=-1).reshape(B, S, nh, hd)
        key = jax.random.key(seed)
        k1, k2, k3, k4, k5 = jax.random.split(key, 5)
        std = 1.0 / np.sqrt(HIDDEN)
        return {'x': jax.random.normal(k1, (2, 256, HIDDEN), dtype=jnp.float32), 'wq': jax.random.normal(k2, (HIDDEN, HIDDEN), dtype=jnp.float32) * std, 'wk': jax.random.normal(k3, (HIDDEN, HIDDEN), dtype=jnp.float32) * std, 'wv': jax.random.normal(k4, (HIDDEN, HIDDEN), dtype=jnp.float32) * std, 'wo': jax.random.normal(k5, (HIDDEN, HIDDEN), dtype=jnp.float32) * std}
    _L0_attn_in = _L0_attn_setup()

    def _L0_ffn_setup():
        import jax, jax.numpy as jnp
        import numpy as np
        key = jax.random.key(seed)
        kx, kw = jax.random.split(key)
        x = jax.random.normal(kx, (32, 512, 128), dtype=jnp.float32)
        weight = jax.random.normal(kw, (128, 128), dtype=jnp.float32) * 0.01
        return {'x': x, 'weight': weight}
    _L0_ffn_in = _L0_ffn_setup()
    _d = {'L0_attn_x': _L0_attn_in['x'], 'L0_attn_wq': _L0_attn_in['wq'], 'L0_attn_wk': _L0_attn_in['wk'], 'L0_attn_wv': _L0_attn_in['wv'], 'L0_attn_wo': _L0_attn_in['wo'], 'L0_ffn_weight': _L0_ffn_in['weight']}
    _x0 = _d['L0_attn_x']
    _d['L0_attn_x'] = jax.random.normal(jax.random.fold_in(jax.random.key(seed), 1), (16, 512, 128), dtype=_x0.dtype)
    del _x0
    return _d

def reference(L0_attn_x, L0_attn_wq, L0_attn_wk, L0_attn_wv, L0_attn_wo, L0_ffn_weight):

    def _L0_attn_ref(x, wq, wk, wv, wo):
        import jax, jax.numpy as jnp
        import numpy as np
        NUM_HEADS = 16
        HIDDEN = 128
        HEAD_DIM = HIDDEN // NUM_HEADS

        def _rope_cos_sin(S, head_dim):
            inv = 1.0 / 10000.0 ** (jnp.arange(0, head_dim, 2, dtype=jnp.float32) / head_dim)
            t = jnp.arange(S, dtype=jnp.float32)
            ang = jnp.outer(t, inv)
            return (jnp.cos(ang), jnp.sin(ang))

        def _apply_rope(x, cos, sin):
            B, S, nh, hd = x.shape
            xr = x[..., 0::2]
            xi = x[..., 1::2]
            c = cos[None, :, None, :]
            s = sin[None, :, None, :]
            or_ = xr * c - xi * s
            oi_ = xr * s + xi * c
            return jnp.stack([or_, oi_], axis=-1).reshape(B, S, nh, hd)
        B, S, H = x.shape
        nh, hd = (NUM_HEADS, HEAD_DIM)
        xq = jnp.einsum('bsh,oh->bso', x, wq).reshape(B, S, nh, hd)
        xk = jnp.einsum('bsh,oh->bso', x, wk).reshape(B, S, nh, hd)
        xv = jnp.einsum('bsh,oh->bso', x, wv).reshape(B, S, nh, hd)
        cos, sin = _rope_cos_sin(S, hd)
        xq = _apply_rope(xq.astype(jnp.float32), cos, sin).astype(x.dtype)
        xk = _apply_rope(xk.astype(jnp.float32), cos, sin).astype(x.dtype)
        scores = jnp.einsum('bqhd,bkhd->bhqk', xq, xk) / np.sqrt(hd)
        probs = jax.nn.softmax(scores.astype(jnp.float32), axis=-1).astype(xq.dtype)
        out = jnp.einsum('bhqk,bkhd->bqhd', probs, xv).reshape(B, S, nh * hd)
        return jnp.einsum('bso,ho->bsh', out, wo)

    def _L0_ffn_ref(x, weight):
        import jax, jax.numpy as jnp
        import numpy as np
        b_weight = jnp.sign(weight)
        return jnp.einsum('bsi,oi->bso', x, b_weight)
    x = L0_attn_x
    x = _layernorm(x + _L0_attn_ref(x, L0_attn_wq, L0_attn_wk, L0_attn_wv, L0_attn_wo), axis=-1)
    x = _layernorm(x + _L0_ffn_ref(x, L0_ffn_weight), axis=-1)
    return x

_drawn_inputs = setup_inputs


def setup_inputs(seed=0):
    import zlib

    import numpy as np

    out = dict(_drawn_inputs(seed))
    spreads = {}
    factors = {}
    for name, (base, spread) in spreads.items():
        noise = np.random.default_rng([zlib.crc32(name.encode()), seed]).standard_normal(out[name].shape)
        drawn = base * np.exp(spread * noise) if base else spread * noise
        out[name] = jnp.asarray(drawn.astype(out[name].dtype))
    for name, factor in factors.items():
        out[name] = (out[name] * factor).astype(out[name].dtype)
    return out
```

```python
from contextlib import ExitStack

import concourse.bass as bass
from concourse import mybir
from concourse.alu_op_type import AluOpType as ALU

BATCH, SEQ, D = 16, 512, 128
HEADS = 16
HD = D // HEADS
P = 128
TILES = SEQ // P
GROUPS = 4
GH = HEADS // GROUPS
STAGES = BATCH * GROUPS
EPS = 1e-5
SCALE = HD ** -0.5

TERMS_Q = [0, 1, 2, 0, 1, 0]
TERMS_K = [0, 0, 0, 1, 1, 2]
TERM_ROWS = len(TERMS_Q) * HD
MAX_ROW = 96
QK_ROWS = MAX_ROW + 3

A_PREP = 8
A_ROPE = 7
A_SPREAD = 4
A_GATHER = 3
A_SMAX = 2
A_MROW = 1
A_DIVIDE = -4
A_WO = -5
A_FFN = -6
A_LN2 = -7


class Step:

    def __init__(self, b, g):
        self.b, self.g = b, g

    def on(self, ahead):
        if not isinstance(self.b, int):
            return True
        return 0 <= GROUPS * self.b + self.g + ahead < STAGES

    def slot(self, ahead):
        return (self.g + ahead) % GROUPS

    def batch(self, ahead):
        return self.b + (self.g + ahead) // GROUPS

    def count(self, ahead, per=1, more=0):
        return self.b * (GROUPS * per) + ((self.g + ahead) * per + more)

    def turn(self, ahead):
        i = self.g + ahead
        return i % 2, self.b * (GROUPS // 2) + (i // 2 + 1)


def some(value):
    return not isinstance(value, int) or value > 0


def body(nc, x, wq_t, wk_t, wv_t, wo_t, wf_t, rope_tab, ident_in, y_out):
    fp32, bf16 = mybir.dt.float32, mybir.dt.bfloat16
    ACT = mybir.ActivationFunctionType
    AX = mybir.AxisListType

    qk_scr = nc.dram_tensor("qk_scr", (2, 2, len(TERMS_Q), HD, GH, GROUPS, SEQ), bf16, kind="Internal").ap()
    o_scr = nc.dram_tensor("o_scr", (2, P, GROUPS, SEQ), fp32, kind="Internal").ap()

    with ExitStack() as ctx:
        def sb(name, shape, dt=fp32):
            return ctx.enter_context(nc.sbuf_tensor(name, shape, dt))

        def ps(name, shape):
            return ctx.enter_context(nc.psum_tensor(name, shape, fp32))

        def sem(name):
            return ctx.enter_context(nc.semaphore(name))

        wq = sb("wq", [P, D])
        wk = sb("wk", [P, D])
        wv = sb("wv", [P, D])
        wo = sb("wo", [P, D])
        wf_raw = sb("wf_raw", [P, D])
        wf_pos = sb("wf_pos", [P, D])
        wf_neg = sb("wf_neg", [P, D])
        wf = sb("wf", [P, D])
        cos_sin = sb("cos_sin", [P, 2, SEQ])
        ident = sb("ident", [P, P])
        ident_b = sb("ident_b", [P, P], bf16)

        x_in = sb("x_in", [P, TILES, D])
        x_t = sb("x_t", [P, 2, P])
        qk_raw = sb("qk_raw", [P, 2, 2, P])
        qk_swap = sb("qk_swap", [P, 2, 2, P])
        rope_a = sb("rope_a", [P, 2, P])
        rope_b = sb("rope_b", [P, 2, P])
        rope_r = sb("rope_r", [P, 2, P])
        rope_rest = sb("rope_rest", [P, 2, P])
        parts = sb("parts", [P, 2, 2, 3, SEQ], bf16)
        v_nat = sb("v_nat", [P, 4, TILES, D])

        q_slot = sb("q_slot", [P, GROUPS, GH, SEQ], bf16)
        k_slot = sb("k_slot", [P, GROUPS, GH, SEQ], bf16)
        v_slot = sb("v_slot", [P, GROUPS, TILES, GH, 32])
        neg_max = sb("neg_max", [P, 2, GH, TILES])
        max_rest = sb("max_rest", [P, GH * TILES])
        max_parts = sb("max_parts", [P, 3, GH * TILES], bf16)
        max_t = sb("max_t", [3 * GH * TILES, P], bf16)
        probs = sb("probs", [P, TILES, GH, SEQ])
        o_sum = sb("o_sum", [P, SEQ])

        att = sb("att", [P, 2, SEQ])
        att_rcp = sb("att_rcp", [P, P])
        att_n = sb("att_n", [P, 2, P])
        x_res = sb("x_res", [P, TILES, D])
        z1 = sb("z1", [P, D])
        st1 = sb("st1", [P, 6])
        mv1 = sb("mv1", [P, 2])
        nr1 = sb("nr1", [P, 2])
        rstd1 = sb("rstd1", [P, 1])
        x2 = sb("x2", [P, 2, D])
        z2 = sb("z2", [P, D])
        st2 = sb("st2", [P, 6])
        mv2 = sb("mv2", [P, 2])
        nr2 = sb("nr2", [P, 2])
        rstd2 = sb("rstd2", [P, 1])
        minus_half = sb("minus_half", [P, 1])
        y = sb("y", [P, TILES, D])

        s_ps = ps("s_ps", [P, 2, 2, SEQ])
        t_ps = ps("t_ps", [P, 2, SEQ])
        o_ps = ps("o_ps", [P, SEQ])
        m_ps = ps("m_ps", [P, SEQ])
        max_t_ps = m_ps[0:3 * GH * TILES, 2 * P:2 * P + P // 2].bitcast(bf16)

        const_in = sem("const_in")
        x_in_done = sem("x_in_done")
        x_res_done = sem("x_res_done")
        swap_done = [sem(f"swap_done{n}") for n in range(2)]
        spread_done = sem("spread_done")
        gather_done = [sem(f"gather_done{n}") for n in range(2)]
        mrow_done = [sem(f"mrow_done{n}") for n in range(2)]
        o_out_done = [sem(f"o_out_done{n}") for n in range(2)]
        att_in_done = sem("att_in_done")
        y_out_done = sem("y_out_done")

        a_full = sem("a_full")
        b_full = sem("b_full")
        c_full = sem("c_full")
        s_full = sem("s_full")
        t_full = sem("t_full")
        pv_done = sem("pv_done")

        a_read = sem("a_read")
        qk_read = sem("qk_read")
        v_read = sem("v_read")
        p_ready = sem("p_ready")
        o_read = sem("o_read")

        setup_v = sem("setup_v")
        s_read = sem("s_read")
        z1_ready = sem("z1_ready")
        st1_ready = sem("st1_ready")
        mv1_ready = sem("mv1_ready")
        ln1_ready = sem("ln1_ready")
        z2_ready = sem("z2_ready")
        st2_ready = sem("st2_ready")
        mv2_ready = sem("mv2_ready")
        ln2_ready = sem("ln2_ready")
        rcp_ready = sem("rcp_ready")

        setup_g = sem("setup_g")
        msplit = sem("msplit")
        rope = sem("rope")
        v_staged = sem("v_staged")
        pow1_ready = sem("pow1_ready")
        pow2_ready = sem("pow2_ready")
        x2_ready = sem("x2_ready")
        att_ready = sem("att_ready")
        y_ready = sem("y_ready")
        waited_s, waited_t, waited_v, waited_g = (sem(f"waited_{n}") for n in "stvg")
        ROPE_STEPS, MSPLIT_STEPS = 8, 4
        CONSTS = 7
        SETUP_G = 7
        SPREAD = 6 * 16

        def phase(b, g):
            return (b + A_PREP // GROUPS) * GROUPS + g + 1

        def run(stage, eng):
            first, last = 2, BATCH - 2 - A_PREP // GROUPS
            for b in range(-A_PREP // GROUPS, first):
                for g in range(GROUPS):
                    stage(Step(b, g))
            with eng.Fori(first, last + 1) as b:
                for g in range(GROUPS):
                    stage(Step(b, g))
            for b in range(last + 1, BATCH + 2):
                for g in range(GROUPS):
                    stage(Step(b, g))

        block = ctx.enter_context(nc.Block())

        @block.sync
        def _(sp):
            def load_batch(buf, done, b):
                sp.dma_start(buf[:, :, :], x[b].rearrange("(t p) d -> p t d", p=P)).then_inc(done, 16)

            sp.dma_start(ident[:, :], ident_in).then_inc(const_in, 16)
            load_batch(x_in, x_in_done, 0)
            for dst, src in ((wq, wq_t), (wk, wk_t), (wv, wv_t), (wo, wo_t), (wf_raw, wf_t)):
                sp.dma_start(dst[:, :], src).then_inc(const_in, 16)
            sp.dma_start(cos_sin[:, :, :], rope_tab).then_inc(const_in, 16)

            def stage(s):
                if s.on(A_GATHER):
                    n, uses = s.turn(A_GATHER)
                    par, g = s.batch(A_GATHER) & 1, s.slot(A_GATHER)
                    if isinstance(s.b, int) and s.count(A_GATHER) == 0:
                        sp.wait_ge(setup_g, SETUP_G)
                        sp.wait_ge(setup_v, 3)
                    sp.wait_ge(spread_done, (s.batch(A_GATHER) + 1) * SPREAD)
                    sp.sem_inc(waited_s, 1)
                    if some(seen := s.count(A_GATHER - GROUPS + 1, GH * TILES)):
                        sp.wait_ge(t_full, seen)
                        sp.sem_inc(waited_s, 1)
                    for side, slot in ((0, q_slot), (1, k_slot)):
                        sp.dma_start(slot[0:TERM_ROWS, g, :, :],
                                     qk_scr[par, side, :, :, :, g, :].rearrange("t r j c -> (t r) j c")) \
                            .then_inc(gather_done[n], 16)
                if s.on(-1):
                    n, uses = s.turn(-1)
                    if some(seen := s.count(-1) + 1):
                        sp.wait_ge(o_read, seen)
                        sp.sem_inc(waited_s, 1)
                    sp.dma_start(o_scr[s.batch(-1) & 1, :, s.slot(-1), :], o_sum[:, :]).then_inc(o_out_done[n], 16)
                if s.g == 0 and s.on(-GROUPS):
                    for n in range(2):
                        if some(seen := s.turn(-2 + n)[1] * 16):
                            sp.wait_ge(o_out_done[n], seen)
                            sp.sem_inc(waited_s, 1)
                    if some(seen := s.count(-GROUPS)):
                        sp.wait_ge(att_ready, seen)
                        sp.sem_inc(waited_s, 1)
                    for j in range(GH):
                        sp.dma_start(
                            att[32 * j:32 * j + 32, :, :],
                            o_scr[s.batch(-GROUPS) & 1, 32 * j:32 * j + 2 * HD, :, :]
                            .rearrange("(n d) g c -> (d g) n c", d=HD),
                        ).then_inc(att_in_done, 16)
                if s.g == 0 and s.on(A_SPREAD):
                    b2 = s.batch(A_SPREAD)
                    sp.wait_ge(rope, (b2 + 1) * (GROUPS * ROPE_STEPS))
                    sp.sem_inc(waited_s, 1)
                    for n in range(2):
                        if some(seen := (b2 - 1) * 64):
                            sp.wait_ge(gather_done[n], seen)
                            sp.sem_inc(waited_s, 1)
                    for side, terms in ((0, TERMS_Q), (1, TERMS_K)):
                        for at, k in ((0, 3), (3, 2), (5, 1)):
                            first = terms[at]
                            if terms[at:at + k] == list(range(first, first + k)):
                                src = parts[:, b2 & 1, side, first:first + k, :]
                            else:
                                src = parts[:, b2 & 1, side, first:first + 1, :].to_broadcast([P, k, SEQ])
                            sp.dma_start(qk_scr[b2 & 1, side, at:at + k].rearrange("t r j g c -> (r j g) t c"), src) \
                                .then_inc(spread_done, 16)
                if s.on(A_MROW):
                    n, uses = s.turn(A_MROW)
                    sp.wait_ge(a_read, phase(s.b, s.g))
                    sp.sem_inc(waited_s, 1)
                    for part in range(3):
                        sp.dma_start(
                            q_slot[MAX_ROW + part:MAX_ROW + part + 1, s.slot(A_MROW), :, :]
                            .rearrange("p j (t c) -> p (j t) c", t=TILES),
                            max_t[part * GH * TILES:(part + 1) * GH * TILES, :],
                        ).then_inc(mrow_done[n], 16)
                if s.g == 0 and s.on(-GROUPS):
                    sp.wait_ge(z1_ready, s.count(A_WO) + 1)
                    sp.sem_inc(waited_s, 1)
                    load_batch(x_res, x_res_done, s.batch(-GROUPS))
                if s.on(A_PREP):
                    n, uses = s.turn(A_PREP)
                    sp.wait_ge(qk_read, s.count(A_PREP) + 1)
                    sp.sem_inc(waited_s, 1)
                    for half in range(2):
                        sp.dma_start(qk_swap[64 * half:64 * half + 64, n, :, :],
                                     qk_raw[64 - 64 * half:128 - 64 * half, n, :, :]).then_inc(swap_done[n], 16)
                if s.g == GROUPS - 1 and s.on(A_PREP + 1):
                    sp.wait_ge(a_full, phase(s.b, s.g))
                    sp.sem_inc(waited_s, 1)
                    load_batch(x_in, x_in_done, s.batch(A_PREP + 1))
                if s.slot(A_LN2) == TILES - 1 and s.on(A_LN2):
                    sp.wait_ge(y_ready, s.count(A_LN2) + 1)
                    sp.sem_inc(waited_s, 1)
                    sp.dma_start(y_out[s.batch(A_LN2)].rearrange("(t p) d -> p t d", p=P), y[:, :, :]) \
                        .then_inc(y_out_done, 16)

            run(stage, sp)
            sp.wait_ge(y_out_done, BATCH * 16)

        @block.tensor
        def _(pe):
            def shifted_scores(s, c, j):
                k = GH * c + j
                if k == 0:
                    n, uses = s.turn(0)
                    pe.wait_ge(mrow_done[n], uses * 48)
                if some(seen := s.count(0, GH * TILES, k - 1)):
                    pe.wait_ge(p_ready, seen)
                pe.matmul(t_ps[:, k % 2, :], k_slot[0:QK_ROWS, s.g, j, P * c:P * c + P],
                          q_slot[0:QK_ROWS, s.g, j, :], start=True, stop=True).then_inc(t_full, 1)

            def score_pair(s, c, jj):
                k = 2 * c + jj
                if k == 0:
                    n, uses = s.turn(A_SMAX)
                    pe.wait_ge(gather_done[n], uses * 32)
                if some(seen := s.count(A_SMAX, 2 * TILES, k - 1)):
                    pe.wait_ge(s_read, seen)
                slot = s.slot(A_SMAX)
                for h in range(2):
                    mm = pe.matmul(s_ps[:, k % 2, h, :], q_slot[0:MAX_ROW, slot, 2 * jj + h, P * c:P * c + P],
                                   k_slot[0:MAX_ROW, slot, 2 * jj + h, :], start=True, stop=True)
                mm.then_inc(s_full, 1)

            def weighted_values(s, ahead, c):
                if c == 0:
                    pe.wait_ge(v_staged, s.count(ahead) + 1)
                    if some(seen := s.count(ahead)):
                        pe.wait_ge(o_read, seen)
                if some(seen := s.count(ahead, GH * TILES, GH * (c + 1))):
                    pe.wait_ge(p_ready, seen)
                for j in range(GH):
                    mm = pe.matmul(o_ps[32 * j:32 * j + 32, :], v_slot[:, s.slot(ahead), c, j, :],
                                   probs[:, c, j, :], start=(c == 0), stop=(c == TILES - 1))
                mm.then_inc(pv_done, 1)

            def phase_a(s):
                if s.on(A_WO):
                    pe.wait_ge(z1_ready, s.count(A_WO) + 1)
                if s.on(A_PREP - 1):
                    if some(seen := s.count(A_PREP - 1) + 1):
                        pe.wait_ge(v_read, seen)
                if s.on(A_FFN - 1):
                    if some(seen := s.count(A_FFN - 1) + 1):
                        pe.wait_ge(z2_ready, seen)
                if s.on(A_PREP):
                    pe.wait_ge(x_in_done, (s.batch(A_PREP) + 1) * 16)
                    mm = pe.transpose(m_ps[:, 0:P], x_in[:, s.slot(A_PREP), :], ident[:, :])
                if s.on(A_FFN):
                    n, uses = s.turn(A_FFN)
                    pe.wait_ge(x2_ready, s.count(A_FFN) + 1)
                    mm = pe.transpose(m_ps[:, P:2 * P], x2[:, n, :], ident[:, :])
                if s.on(A_MROW):
                    if some(seen := s.count(A_MROW, MSPLIT_STEPS, MSPLIT_STEPS)):
                        pe.wait_ge(msplit, seen)
                        pe.sem_inc(waited_t, 1)
                    mm = pe.transpose(max_t_ps, max_parts[:, :, :].rearrange("p a m -> p (a m)"), ident_b[:, :])
                mm.then_inc(a_full, 1)

            def phase_b(s):
                pe.wait_ge(a_read, phase(s.b, s.g))
                if s.on(A_PREP):
                    pe.matmul(m_ps[:, 0:P], wq[:, :], x_t[:, 0, :], start=True, stop=True)
                    pe.matmul(m_ps[:, P:2 * P], wk[:, :], x_t[:, 0, :], start=True, stop=True)
                    mm = pe.matmul(m_ps[:, 2 * P:3 * P], x_t[:, 0, :], wv[:, :], start=True, stop=True)
                if s.on(A_FFN):
                    mm = pe.matmul(m_ps[:, 3 * P:4 * P], x_t[:, 1, :], wf[:, :], start=True, stop=True)
                mm.then_inc(b_full, 1)

            def phase_c(s):
                if s.on(A_PREP - 1):
                    if some(seen := s.count(A_PREP - 1) + 1):
                        pe.wait_ge(v_read, seen)
                if s.on(A_FFN - 1):
                    if some(seen := s.count(A_FFN - 1) + 1):
                        pe.wait_ge(z2_ready, seen)
                pe.wait_ge(att_ready, s.count(A_WO) + 1)
                pe.matmul(m_ps[:, 0:P], att_n[:, s.turn(A_WO)[0], :], wo[:, :], start=True, stop=True).then_inc(c_full, 1)

            pe.wait_ge(const_in, CONSTS * 16)
            pe.wait_ge(setup_v, 3)
            pe.wait_ge(setup_g, SETUP_G)

            def stage(s):
                for c in range(TILES):
                    for jj in range(2):
                        if s.on(0):
                            shifted_scores(s, c, 2 * jj)
                        if s.on(A_SMAX):
                            score_pair(s, c, jj)
                        if s.on(0):
                            shifted_scores(s, c, 2 * jj + 1)
                        if jj == 0:
                            if c == 0 and s.on(-1):
                                weighted_values(s, -1, TILES - 1)
                            if c > 0 and s.on(0):
                                weighted_values(s, 0, c - 1)
                    if c == 0 and s.on(A_WO):
                        phase_c(s)
                    if c == 1 and (s.on(A_PREP) or s.on(A_FFN) or s.on(A_MROW)):
                        phase_a(s)
                    if c == 2 and (s.on(A_PREP) or s.on(A_FFN)):
                        phase_b(s)

            run(stage, pe)

        @block.scalar
        def _(act):
            def exp(s, c, j):
                k = GH * c + j
                if some(seen := s.count(0, GH * TILES, k + 1)):
                    act.wait_ge(t_full, seen)
                if j == 0:
                    if some(seen := s.count(-1, TILES, c + 1)):
                        act.wait_ge(pv_done, seen)
                act.activation(probs[:, c, j, :], t_ps[:, k % 2, :], ACT.Exp, scale=SCALE).then_inc(p_ready, 1)

            def sums_out(s):
                if some(seen := s.count(-1, TILES, TILES)):
                    act.wait_ge(pv_done, seen)
                if s.on(-2):
                    n, uses = s.turn(-2)
                    act.wait_ge(o_out_done[n], uses * 16)
                act.copy(o_sum[:, :], o_ps[:, :]).then_inc(o_read, 1)

            def phase_a_out(s):
                act.wait_ge(a_full, phase(s.b, s.g))
                lo, hi = (0 if s.on(A_PREP) else 1), (2 if s.on(A_FFN) else 1)
                last = None
                if s.on(A_PREP) or s.on(A_FFN):
                    last = act.copy(x_t[:, lo:hi, :], m_ps[:, P * lo:P * hi].rearrange("p (a c) -> p a c", c=P))
                if s.on(A_MROW):
                    n, uses = s.turn(A_MROW - 1)
                    if s.on(A_MROW - 1):
                        act.wait_ge(mrow_done[n], uses * 48)
                    last = act.copy(max_t[:, :], max_t_ps)
                last.then_inc(a_read, 1)

            def phase_b_out(s):
                n, uses = s.turn(A_PREP)
                act.wait_ge(b_full, phase(s.b, s.g))
                if some(seen := s.count(A_PREP - 2, ROPE_STEPS, ROPE_STEPS)):
                    act.wait_ge(rope, seen)
                if s.on(A_PREP - 2):
                    m, uses = s.turn(A_PREP - 2)
                    act.wait_ge(swap_done[m], uses * 32)
                act.copy(qk_raw[:, n, :, :], m_ps[:, 0:2 * P].rearrange("p (a c) -> p a c", c=P)).then_inc(qk_read, 1)
                act.copy(v_nat[:, s.batch(A_PREP) & 3, s.slot(A_PREP), :], m_ps[:, 2 * P:3 * P]).then_inc(v_read, 1)

            def stage(s):
                for c in range(TILES):
                    for j in range(GH):
                        if s.on(0):
                            exp(s, c, j)
                        if c == 0 and j == 3 and s.on(-1):
                            sums_out(s)
                        if c == 2 and j == 1 and (s.on(A_PREP) or s.on(A_FFN) or s.on(A_MROW)):
                            phase_a_out(s)
                        if c == 3 and j == 1 and s.on(A_PREP):
                            phase_b_out(s)

            run(stage, act)

        @block.vector
        def _(dve):
            dve.memset(q_slot[:, :, :, :].bitcast(fp32), 0.0).then_inc(setup_v, 1)
            dve.wait_ge(const_in, CONSTS * 16)
            dve.tensor_scalar(wf_pos[:, :], wf_raw[:, :], 0.0, None, ALU.is_gt)
            dve.tensor_scalar(wf_neg[:, :], wf_raw[:, :], 0.0, None, ALU.is_lt).then_inc(setup_v, 1)
            dve.wait_ge(setup_v, 2)
            dve.tensor_tensor(wf[:, :], wf_pos[:, :], wf_neg[:, :], ALU.subtract).then_inc(setup_v, 1)

            def pair_max(s, k):
                c, jj = k // 2, k % 2
                if k == 0:
                    if some(seen := s.count(A_SMAX - 2, MSPLIT_STEPS, MSPLIT_STEPS)):
                        dve.wait_ge(msplit, seen)
                if some(seen := s.count(A_SMAX, 2 * TILES, k + 1)):
                    dve.wait_ge(s_full, seen)
                dve.tensor_reduce(neg_max[:, s.turn(A_SMAX)[0], 2 * jj:2 * jj + 2, c], s_ps[:, k % 2, :, :],
                                  AX.X, ALU.max, negate=True).then_inc(s_read, 1)

            def add_first(s, ahead):
                dve.wait_ge(c_full, s.count(ahead) + 1)
                dve.wait_ge(x_res_done, (s.batch(ahead) + 1) * 16)
                if some(seen := s.count(ahead - 1) + 1):
                    dve.wait_ge(x2_ready, seen)
                dve.tensor_tensor(z1[:, :], m_ps[:, 0:P], x_res[:, s.slot(ahead), :], ALU.add).then_inc(z1_ready, 1)

            def add_second(s, ahead):
                n, uses = s.turn(ahead)
                dve.wait_ge(b_full, phase(s.b, s.g))
                if s.on(A_PREP):
                    dve.wait_ge(v_read, s.count(A_PREP) + 1)
                if some(seen := s.count(ahead - 1) + 1):
                    dve.wait_ge(y_ready, seen)
                dve.tensor_tensor(z2[:, :], m_ps[:, 3 * P:4 * P], x2[:, n, :], ALU.add).then_inc(z2_ready, 1)

            def stats(s, ahead, z, st, ready, done):
                dve.wait_ge(ready, s.count(ahead) + 1)
                dve.bn_stats(st[:, :], z[:, :]).then_inc(done, 1)

            def moments(s, ahead, st, mv, ready, done):
                dve.wait_ge(ready, s.count(ahead) + 1)
                dve.sem_inc(waited_v, 1)
                dve.bn_aggr(mv[:, :], st[:, :]).then_inc(done, 1)

            def factors(s, ahead, mv, nr, ready, done):
                dve.wait_ge(ready, s.count(ahead) + 1)
                dve.tensor_scalar(nr[:, 0:1], mv[:, 0:1], -1.0, None, ALU.mult)
                dve.tensor_scalar(nr[:, 1:2], mv[:, 1:2], EPS, None, ALU.add).then_inc(done, 1)

            def reciprocals(s):
                dve.wait_ge(att_in_done, (s.batch(A_DIVIDE) + 1) * (GH * 16))
                if some(seen := s.count(A_DIVIDE)):
                    dve.wait_ge(att_ready, seen)
                t = s.slot(A_DIVIDE)
                dve.reciprocal(att_rcp[:, :], att[:, 1, P * t:P * t + P]).then_inc(rcp_ready, 1)

            def stage(s):
                for k in range(2 * TILES):
                    if s.on(A_SMAX):
                        pair_max(s, k)
                    if k == 0 and s.on(A_LN2):
                        stats(s, A_LN2, z2, st2, z2_ready, st2_ready)
                    if k == 1 and s.on(A_LN2):
                        moments(s, A_LN2, st2, mv2, st2_ready, mv2_ready)
                    if k == 2 and s.on(A_LN2):
                        factors(s, A_LN2, mv2, nr2, mv2_ready, ln2_ready)
                    if k == 2 and s.on(A_WO):
                        add_first(s, A_WO)
                    if k == 3 and s.on(A_WO):
                        stats(s, A_WO, z1, st1, z1_ready, st1_ready)
                    if k == 4 and s.on(A_WO):
                        moments(s, A_WO, st1, mv1, st1_ready, mv1_ready)
                        factors(s, A_WO, mv1, nr1, mv1_ready, ln1_ready)
                    if k == 5 and s.on(A_DIVIDE):
                        reciprocals(s)
                    if k == 7 and s.on(A_FFN):
                        add_second(s, A_FFN)

            run(stage, dve)

        @block.gpsimd
        def _(pool):
            pool.memset(k_slot[:, :, :, :].bitcast(fp32), 0.0).then_inc(setup_g, 1)
            pool.wait_ge(setup_g, 1)
            pool.memset(k_slot[MAX_ROW:QK_ROWS, :, :, :], 1.0).then_inc(setup_g, 1)
            pool.wait_ge(setup_g, 2)
            pool.memset(minus_half[:, :], -0.5).then_inc(setup_g, 1)
            pool.memset(v_slot[:, :, :, :, HD:2 * HD], 1.0).then_inc(setup_g, 1)
            pool.memset(v_slot[:, :, :, :, 2 * HD:32], 0.0).then_inc(setup_g, 1)
            pool.wait_ge(setup_g, 5)
            pool.wait_ge(const_in, CONSTS * 16)
            pool.tensor_copy(ident_b[:, :], ident[:, :]).then_inc(setup_g, 2)

            def split_maxima(s):
                n, _ = s.turn(A_MROW)
                m = neg_max[:, n, :, :].rearrange("p j t -> p (j t)")
                at = lambda k: s.count(A_MROW, MSPLIT_STEPS, k)
                if some(seen := s.count(A_MROW, 2 * TILES, 2 * TILES)):
                    pool.wait_ge(s_read, seen)
                    pool.sem_inc(waited_g, 1)
                if some(seen := phase(s.b, s.g) - 1):
                    pool.wait_ge(a_full, seen)
                    pool.sem_inc(waited_g, 1)
                pool.tensor_copy(max_parts[:, 0, :], m).then_inc(msplit, 1)
                if some(seen := at(1)):
                    pool.wait_ge(msplit, seen)
                    pool.sem_inc(waited_g, 1)
                pool.tensor_tensor(max_rest[:, :], m, max_parts[:, 0, :], ALU.subtract).then_inc(msplit, 1)
                if some(seen := at(2)):
                    pool.wait_ge(msplit, seen)
                    pool.sem_inc(waited_g, 1)
                pool.tensor_copy(max_parts[:, 1, :], max_rest[:, :]).then_inc(msplit, 1)
                if some(seen := at(3)):
                    pool.wait_ge(msplit, seen)
                    pool.sem_inc(waited_g, 1)
                pool.tensor_tensor(max_parts[:, 2, :], max_rest[:, :], max_parts[:, 1, :], ALU.subtract).then_inc(msplit, 1)

            def rotate(s):
                n, uses = s.turn(A_ROPE)
                t = s.slot(A_ROPE)
                tab = lambda k: cos_sin[:, k:k + 1, P * t:P * t + P].to_broadcast([P, 2, P])
                at = lambda k: s.count(A_ROPE, ROPE_STEPS, k)
                pool.wait_ge(qk_read, s.count(A_ROPE) + 1)
                pool.sem_inc(waited_g, 1)
                pool.tensor_tensor(rope_a[:, :, :], qk_raw[:, n, :, :], tab(0), ALU.mult).then_inc(rope, 1)
                pool.wait_ge(swap_done[n], uses * 32)
                pool.sem_inc(waited_g, 1)
                pool.tensor_tensor(rope_b[:, :, :], qk_swap[:, n, :, :], tab(1), ALU.mult).then_inc(rope, 1)
                if some(seen := at(2)):
                    pool.wait_ge(rope, seen)
                    pool.sem_inc(waited_g, 1)
                pool.tensor_tensor(rope_r[:, :, :], rope_a[:, :, :], rope_b[:, :, :], ALU.add).then_inc(rope, 1)

            def split_rotated(s):
                t = s.slot(A_ROPE)
                b2 = s.batch(A_ROPE)
                part = lambda k: parts[:, b2 & 1, :, k, P * t:P * t + P]
                at = lambda k: s.count(A_ROPE, ROPE_STEPS, k)
                if t == 0:
                    if some(seen := (b2 - 1) * SPREAD):
                        pool.wait_ge(spread_done, seen)
                        pool.sem_inc(waited_g, 1)
                if some(seen := at(3)):
                    pool.wait_ge(rope, seen)
                    pool.sem_inc(waited_g, 1)
                pool.tensor_copy(part(0), rope_r[:, :, :]).then_inc(rope, 1)
                if some(seen := at(4)):
                    pool.wait_ge(rope, seen)
                    pool.sem_inc(waited_g, 1)
                pool.tensor_tensor(rope_rest[:, :, :], rope_r[:, :, :], part(0), ALU.subtract).then_inc(rope, 1)
                if some(seen := at(5)):
                    pool.wait_ge(rope, seen)
                    pool.sem_inc(waited_g, 1)
                pool.tensor_copy(part(1), rope_rest[:, :, :]).then_inc(rope, 1)
                if some(seen := at(6)):
                    pool.wait_ge(rope, seen)
                    pool.sem_inc(waited_g, 1)
                pool.tensor_tensor(part(2), rope_rest[:, :, :], part(1), ALU.subtract).then_inc(rope, 2)

            def stage_values(s):
                g = s.slot(A_MROW)
                b2 = s.batch(A_MROW)
                pool.wait_ge(v_read, (b2 + 1) * TILES)
                pool.sem_inc(waited_g, 1)
                if some(seen := s.count(A_MROW - GROUPS, TILES, TILES)):
                    pool.wait_ge(pv_done, seen)
                    pool.sem_inc(waited_g, 1)
                pool.tensor_copy(v_slot[:, g, :, :, 0:HD],
                                 v_nat[:, b2 & 3, :, 32 * g:32 * g + 32].rearrange("p t (j d) -> p t j d", d=HD)) \
                    .then_inc(v_staged, 1)

            def normalise(s, ahead, z, nr, rstd, out, ready, powered, done):
                pool.wait_ge(ready, s.count(ahead) + 1)
                pool.sem_inc(waited_g, 1)
                pool.tensor_tensor(rstd[:, :], nr[:, 1:2], minus_half[:, :], ALU.pow).then_inc(powered, 1)
                pool.wait_ge(powered, s.count(ahead) + 1)
                pool.sem_inc(waited_g, 1)
                pool.tensor_scalar(out, z[:, :], nr[:, 0:1], rstd[:, :], ALU.add, ALU.mult).then_inc(done, 1)

            def divide(s):
                t = s.slot(A_DIVIDE)
                pool.wait_ge(rcp_ready, s.count(A_DIVIDE) + 1)
                pool.sem_inc(waited_g, 1)
                if some(seen := s.count(A_DIVIDE - 1)):
                    pool.wait_ge(c_full, seen)
                    pool.sem_inc(waited_g, 1)
                pool.tensor_tensor(att_n[:, s.turn(A_DIVIDE)[0], :], att[:, 0, P * t:P * t + P], att_rcp[:, :], ALU.mult) \
                    .then_inc(att_ready, 1)

            def stage(s):
                if s.on(A_MROW):
                    split_maxima(s)
                if s.on(A_ROPE):
                    rotate(s)
                    split_rotated(s)
                if s.on(A_LN2):
                    if s.slot(A_LN2) == 0:
                        if some(seen := s.batch(A_LN2) * 16):
                            pool.wait_ge(y_out_done, seen)
                            pool.sem_inc(waited_g, 1)
                    normalise(s, A_LN2, z2, nr2, rstd2, y[:, s.slot(A_LN2), :], ln2_ready, pow2_ready, y_ready)
                if s.on(A_MROW):
                    stage_values(s)
                if s.on(A_WO):
                    if some(seen := s.count(A_WO - 2) + 1):
                        pool.wait_ge(z2_ready, seen)
                        pool.sem_inc(waited_g, 1)
                    normalise(s, A_WO, z1, nr1, rstd1, x2[:, s.turn(A_WO)[0], :], ln1_ready, pow1_ready, x2_ready)
                if s.on(A_DIVIDE):
                    divide(s)

            run(stage, pool)


def rope_table():
    import numpy as np
    inv = (np.float32(1.0) / np.power(np.float32(10000.0), np.arange(0, HD, 2, dtype=np.float32) / np.float32(HD))).astype(np.float32)
    ang = (np.arange(SEQ, dtype=np.float32)[None, :] * inv[:, None]).astype(np.float32)
    cos, sin = np.cos(ang).astype(np.float32), np.sin(ang).astype(np.float32)
    tab = np.zeros((2, HD // 2, HEADS, 2, SEQ), np.float32)
    tab[:, :, :, 0, :] = cos[None, :, None, :]
    tab[0, :, :, 1, :] = -sin[:, None, :]
    tab[1, :, :, 1, :] = sin[:, None, :]
    return tab.reshape(P, 2, SEQ)


def kernel(**inputs):
    import numpy as np
    import concourse.bacc as bacc
    from concourse.bass_utils import run_bass_kernel_spmd

    def rows_of_qk(w):
        w = w.reshape(GROUPS, GH, HD // 2, 2, D).transpose(3, 2, 1, 0, 4).reshape(D, D)
        return np.ascontiguousarray(w.T)

    a = {k: np.asarray(v) for k, v in inputs.items()}
    wo_rows = a["L0_attn_wo"].T.reshape(GROUPS, GH, HD, D).transpose(1, 2, 0, 3).reshape(D, D)
    arrays = {
        "x": np.ascontiguousarray(a["L0_attn_x"]),
        "wq_t": rows_of_qk(a["L0_attn_wq"]),
        "wk_t": rows_of_qk(a["L0_attn_wk"]),
        "wv_t": np.ascontiguousarray(a["L0_attn_wv"].T),
        "wo_t": np.ascontiguousarray(wo_rows),
        "wf_t": np.ascontiguousarray(a["L0_ffn_weight"].T),
        "rope_tab": rope_table(),
        "ident_in": np.eye(P, dtype=np.float32),
    }
    nc = bacc.Bacc("TRN2", target_bir_lowering=False, num_devices=1)
    args = [nc.dram_tensor(k, v.shape, mybir.dt.from_np(v.dtype), kind="ExternalInput").ap() for k, v in arrays.items()]
    out = nc.dram_tensor("y_out", (BATCH, SEQ, D), mybir.dt.float32, kind="ExternalOutput").ap()
    body(nc, *args, out)
    r = run_bass_kernel_spmd(nc, [arrays], core_ids=[0])
    return r.results[0]["y_out"]
```

```python
from contextlib import ExitStack

import concourse.bass as bass
import numpy as np
from concourse import mybir
from concourse.alu_op_type import AluOpType as ALU

BATCH, SEQ, D = 16, 512, 128
HEADS = 16
HD = D // HEADS
P = 128
TILES = SEQ // P
GROUPS = 4
GH = HEADS // GROUPS
STAGES = BATCH * GROUPS
EPS = 1e-5
SCALE = HD ** -0.5

TERMS_Q = [0, 1, 2, 0, 1, 0]
TERMS_K = [0, 0, 0, 1, 1, 2]
TERM_ROWS = len(TERMS_Q) * HD
MAX_ROW = 96
QK_ROWS = MAX_ROW + 3

A_PREP = 9
A_ROPE = 8
A_GATHER = 3
A_SMAX = 2
A_MROW = 1
A_DIVIDE = -5
A_WO = -6
A_FFN = -7
A_LN2 = -8


class Step:

    def __init__(self, b, g):
        self.b, self.g = b, g

    def on(self, ahead):
        if not isinstance(self.b, int):
            return True
        return 0 <= GROUPS * self.b + self.g + ahead < STAGES

    def slot(self, ahead):
        return (self.g + ahead) % GROUPS

    def batch(self, ahead):
        return self.b + (self.g + ahead) // GROUPS

    def count(self, ahead, per=1, more=0):
        return self.b * (GROUPS * per) + ((self.g + ahead) * per + more)

    def turn(self, ahead):
        i = self.g + ahead
        return i % 2, self.b * (GROUPS // 2) + (i // 2 + 1)


def some(value):
    return not isinstance(value, int) or value > 0


def body(nc, x, wq_t, wk_t, wv_t, wo_t, wf_t, rope_tab, ident_in, y_out):
    fp32, bf16 = mybir.dt.float32, mybir.dt.bfloat16
    ACT = mybir.ActivationFunctionType
    AX = mybir.AxisListType

    qk_scr = nc.dram_tensor("qk_scr", (2, 2, len(TERMS_Q), HD, GH, GROUPS, SEQ), bf16, kind="Internal").ap()
    o_scr = nc.dram_tensor("o_scr", (2, P, GROUPS, SEQ), fp32, kind="Internal").ap()

    with ExitStack() as ctx:
        def sb(name, shape, dt=fp32):
            return ctx.enter_context(nc.sbuf_tensor(name, shape, dt))

        def ps(name, shape):
            return ctx.enter_context(nc.psum_tensor(name, shape, fp32))

        def sem(name):
            return ctx.enter_context(nc.semaphore(name))

        wq = sb("wq", [P, D])
        wk = sb("wk", [P, D])
        wv = sb("wv", [P, D])
        wo = sb("wo", [P, D])
        wf_raw = sb("wf_raw", [P, D])
        wf_pos = sb("wf_pos", [P, D])
        wf_neg = sb("wf_neg", [P, D])
        wf = sb("wf", [P, D])
        cos_sin = sb("cos_sin", [P, 2, SEQ])
        ident = sb("ident", [P, P])
        ident_b = sb("ident_b", [P, P], bf16)

        x_in = sb("x_in", [P, TILES, D])
        x_t = sb("x_t", [P, 2, P])
        qk_raw = sb("qk_raw", [P, 2, 2, P])
        qk_swap = sb("qk_swap", [P, 2, 2, P])
        rope_a = sb("rope_a", [P, 2, P])
        rope_b = sb("rope_b", [P, 2, P])
        rope_r = sb("rope_r", [P, 2, P])
        rope_rest = sb("rope_rest", [P, 2, P])
        parts = sb("parts", [P, 2, 2, 3, SEQ], bf16)
        v_nat = sb("v_nat", [P, 4, TILES, D])

        q_slot = sb("q_slot", [P, GROUPS, GH, SEQ], bf16)
        k_slot = sb("k_slot", [P, GROUPS, GH, SEQ], bf16)
        v_slot = sb("v_slot", [P, GROUPS, TILES, GH, 32])
        neg_max = sb("neg_max", [P, 2, GH, TILES])
        max_rest = sb("max_rest", [P, GH * TILES])
        max_parts = sb("max_parts", [P, 3, GH * TILES], bf16)
        max_t = sb("max_t", [3 * GH * TILES, P], bf16)
        probs = sb("probs", [P, TILES, GH, SEQ])
        o_sum = sb("o_sum", [P, SEQ])

        att = sb("att", [P, 2, SEQ])
        att_rcp = sb("att_rcp", [P, P])
        att_n = sb("att_n", [P, 2, P])
        x_res = sb("x_res", [P, TILES, D])
        z1 = sb("z1", [P, D])
        st1 = sb("st1", [P, 6])
        mv1 = sb("mv1", [P, 2])
        nr1 = sb("nr1", [P, 2])
        rstd1 = sb("rstd1", [P, 1])
        x2 = sb("x2", [P, 2, D])
        z2 = sb("z2", [P, D])
        st2 = sb("st2", [P, 6])
        mv2 = sb("mv2", [P, 2])
        nr2 = sb("nr2", [P, 2])
        rstd2 = sb("rstd2", [P, 1])
        minus_half = sb("minus_half", [P, 1])
        y = sb("y", [P, TILES, D])

        s_ps = ps("s_ps", [P, 2, 2, SEQ])
        t_ps = ps("t_ps", [P, 2, SEQ])
        o_ps = ps("o_ps", [P, SEQ])
        m_ps = ps("m_ps", [P, SEQ])
        max_t_ps = m_ps[0:3 * GH * TILES, 2 * P:2 * P + P // 2].bitcast(bf16)

        ident_done = sem("ident_done")
        wqkv_in = sem("wqkv_in")
        table_in = sem("table_in")
        wf_wo_in = sem("wf_wo_in")
        x_in_done = sem("x_in_done")
        x_res_done = sem("x_res_done")
        swap_done = [sem(f"swap_done{n}") for n in range(2)]
        spread_done = sem("spread_done")
        gather_done = [sem(f"gather_done{n}") for n in range(2)]
        mrow_done = [sem(f"mrow_done{n}") for n in range(2)]
        o_out_done = [sem(f"o_out_done{n}") for n in range(2)]
        att_in_done = sem("att_in_done")
        y_out_done = sem("y_out_done")

        a_full = sem("a_full")
        b_full = sem("b_full")
        c_full = sem("c_full")
        s_full = sem("s_full")
        t_full = sem("t_full")
        pv_done = sem("pv_done")

        a_read = sem("a_read")
        qk_read = sem("qk_read")
        v_read = sem("v_read")
        p_ready = sem("p_ready")
        o_read = sem("o_read")

        setup_v = sem("setup_v")
        s_read = sem("s_read")
        z1_ready = sem("z1_ready")
        st1_ready = sem("st1_ready")
        mv1_ready = sem("mv1_ready")
        ln1_ready = sem("ln1_ready")
        z2_ready = sem("z2_ready")
        st2_ready = sem("st2_ready")
        mv2_ready = sem("mv2_ready")
        ln2_ready = sem("ln2_ready")
        rcp_ready = sem("rcp_ready")

        setup_g = sem("setup_g")
        msplit = sem("msplit")
        rope = sem("rope")
        v_staged = sem("v_staged")
        pow1_ready = sem("pow1_ready")
        pow2_ready = sem("pow2_ready")
        x2_ready = sem("x2_ready")
        att_ready = sem("att_ready")
        y_ready = sem("y_ready")
        waited_s, waited_t, waited_v, waited_g = (sem(f"waited_{n}") for n in "stvg")
        ROPE_STEPS, MSPLIT_STEPS = 8, 4
        SETUP_G = 8
        SETUP_V = 2
        SPREAD = 6 * 16

        def phase(b, g):
            return b * GROUPS + (g + A_PREP + 1)

        def rotate(eng, own, s):
            n, uses = s.turn(A_ROPE)
            t = s.slot(A_ROPE)
            tab = lambda k: cos_sin[:, k:k + 1, P * t:P * t + P].to_broadcast([P, 2, P])
            at = lambda k: s.count(A_ROPE, ROPE_STEPS, k)
            eng.wait_ge(qk_read, s.count(A_ROPE) + 1)
            eng.sem_inc(own, 1)
            eng.tensor_tensor(rope_a[:, :, :], qk_raw[:, n, :, :], tab(0), ALU.mult).then_inc(rope, 1)
            eng.wait_ge(swap_done[n], uses * 32)
            eng.sem_inc(own, 1)
            eng.tensor_tensor(rope_b[:, :, :], qk_swap[:, n, :, :], tab(1), ALU.mult).then_inc(rope, 1)
            if some(seen := at(2)):
                eng.wait_ge(rope, seen)
                eng.sem_inc(own, 1)
            eng.tensor_tensor(rope_r[:, :, :], rope_a[:, :, :], rope_b[:, :, :], ALU.add).then_inc(rope, 1)

        def split_rotated(eng, own, s):
            t = s.slot(A_ROPE)
            b2 = s.batch(A_ROPE)
            part = lambda k: parts[:, b2 & 1, :, k, P * t:P * t + P]
            at = lambda k: s.count(A_ROPE, ROPE_STEPS, k)
            if t == 0:
                if some(seen := (b2 - 1) * SPREAD):
                    eng.wait_ge(spread_done, seen)
                    eng.sem_inc(own, 1)
            if some(seen := at(3)):
                eng.wait_ge(rope, seen)
                eng.sem_inc(own, 1)
            eng.tensor_copy(part(0), rope_r[:, :, :]).then_inc(rope, 1)
            if some(seen := at(4)):
                eng.wait_ge(rope, seen)
                eng.sem_inc(own, 1)
            eng.tensor_tensor(rope_rest[:, :, :], rope_r[:, :, :], part(0), ALU.subtract).then_inc(rope, 1)
            if some(seen := at(5)):
                eng.wait_ge(rope, seen)
                eng.sem_inc(own, 1)
            eng.tensor_copy(part(1), rope_rest[:, :, :]).then_inc(rope, 1)
            if some(seen := at(6)):
                eng.wait_ge(rope, seen)
                eng.sem_inc(own, 1)
            eng.tensor_tensor(part(2), rope_rest[:, :, :], part(1), ALU.subtract).then_inc(rope, 2)

        def run(stage, eng):
            first, last = 2, BATCH - 2 - A_PREP // GROUPS
            for b in range(-A_PREP // GROUPS, first):
                for g in range(GROUPS):
                    stage(Step(b, g))
            with eng.Fori(first, last + 1) as b:
                for g in range(GROUPS):
                    stage(Step(b, g))
            for b in range(last + 1, BATCH + 3):
                for g in range(GROUPS):
                    stage(Step(b, g))

        block = ctx.enter_context(nc.Block())

        @block.sync
        def _(sp):
            def load_batch(buf, done, b):
                sp.dma_start(buf[:, :, :], x[b].rearrange("(t p) d -> p t d", p=P)).then_inc(done, 16)

            sp.dma_start(ident[:, :], ident_in).then_inc(ident_done, 16)
            load_batch(x_in, x_in_done, 0)
            for dst, src in ((wq, wq_t), (wk, wk_t), (wv, wv_t)):
                sp.dma_start(dst[:, :], src).then_inc(wqkv_in, 16)
            sp.dma_start(cos_sin[:, :, :], rope_tab).then_inc(table_in, 16)
            for dst, src in ((wf_raw, wf_t), (wo, wo_t)):
                sp.dma_start(dst[:, :], src).then_inc(wf_wo_in, 16)

            def stage(s):
                if s.on(A_GATHER):
                    n, uses = s.turn(A_GATHER)
                    par, g = s.batch(A_GATHER) & 1, s.slot(A_GATHER)
                    if isinstance(s.b, int) and s.count(A_GATHER) == 0:
                        sp.wait_ge(setup_g, SETUP_G)
                    sp.wait_ge(spread_done, (s.batch(A_GATHER) + 1) * SPREAD)
                    sp.sem_inc(waited_s, 1)
                    if some(seen := s.count(A_GATHER - GROUPS + 1, GH * TILES)):
                        sp.wait_ge(t_full, seen)
                        sp.sem_inc(waited_s, 1)
                    for side, slot in ((0, q_slot), (1, k_slot)):
                        sp.dma_start(slot[0:TERM_ROWS, g, :, :],
                                     qk_scr[par, side, :, :, :, g, :].rearrange("t r j c -> (t r) j c")) \
                            .then_inc(gather_done[n], 16)
                if s.on(-1):
                    n, uses = s.turn(-1)
                    if some(seen := s.count(-1) + 1):
                        sp.wait_ge(o_read, seen)
                        sp.sem_inc(waited_s, 1)
                    sp.dma_start(o_scr[s.batch(-1) & 1, :, s.slot(-1), :], o_sum[:, :]).then_inc(o_out_done[n], 16)
                if s.on(A_MROW):
                    n, uses = s.turn(A_MROW)
                    sp.wait_ge(a_read, phase(s.b, s.g))
                    sp.sem_inc(waited_s, 1)
                    for part in range(3):
                        sp.dma_start(
                            q_slot[MAX_ROW + part:MAX_ROW + part + 1, s.slot(A_MROW), :, :]
                            .rearrange("p j (t c) -> p (j t) c", t=TILES),
                            max_t[part * GH * TILES:(part + 1) * GH * TILES, :],
                        ).then_inc(mrow_done[n], 16)
                if s.g == 0 and s.on(-GROUPS):
                    for n in range(2):
                        if some(seen := s.turn(-2 + n)[1] * 16):
                            sp.wait_ge(o_out_done[n], seen)
                            sp.sem_inc(waited_s, 1)
                    if some(seen := s.count(-GROUPS)):
                        sp.wait_ge(att_ready, seen)
                        sp.sem_inc(waited_s, 1)
                    for j in range(GH):
                        sp.dma_start(
                            att[32 * j:32 * j + 32, :, :],
                            o_scr[s.batch(-GROUPS) & 1, 32 * j:32 * j + 2 * HD, :, :]
                            .rearrange("(n d) g c -> (d g) n c", d=HD),
                        ).then_inc(att_in_done, 16)
                if s.slot(A_WO) == TILES - 1 and s.on(A_WO + 1):
                    if some(seen := s.count(A_WO) + 1):
                        sp.wait_ge(z1_ready, seen)
                        sp.sem_inc(waited_s, 1)
                    load_batch(x_res, x_res_done, s.batch(A_WO + 1))
                if s.slot(A_PREP) == TILES - 1 and s.on(A_PREP) and s.on(A_PREP + 1):
                    sp.wait_ge(a_full, phase(s.b, s.g))
                    sp.sem_inc(waited_s, 1)
                    load_batch(x_in, x_in_done, s.batch(A_PREP + 1))
                if s.on(A_PREP):
                    n, uses = s.turn(A_PREP)
                    sp.wait_ge(qk_read, s.count(A_PREP) + 1)
                    sp.sem_inc(waited_s, 1)
                    for half in range(2):
                        sp.dma_start(qk_swap[64 * half:64 * half + 64, n, :, :],
                                     qk_raw[64 - 64 * half:128 - 64 * half, n, :, :]).then_inc(swap_done[n], 16)
                if s.slot(A_ROPE) == TILES - 1 and s.on(A_ROPE):
                    b2 = s.batch(A_ROPE)
                    sp.wait_ge(rope, (b2 + 1) * (GROUPS * ROPE_STEPS))
                    sp.sem_inc(waited_s, 1)
                    for n in range(2):
                        if some(seen := (b2 - 1) * 64):
                            sp.wait_ge(gather_done[n], seen)
                            sp.sem_inc(waited_s, 1)
                    for side, terms in ((0, TERMS_Q), (1, TERMS_K)):
                        for at, k in ((0, 3), (3, 2), (5, 1)):
                            first = terms[at]
                            if terms[at:at + k] == list(range(first, first + k)):
                                src = parts[:, b2 & 1, side, first:first + k, :]
                            else:
                                src = parts[:, b2 & 1, side, first:first + 1, :].to_broadcast([P, k, SEQ])
                            sp.dma_start(qk_scr[b2 & 1, side, at:at + k].rearrange("t r j g c -> (r j g) t c"), src) \
                                .then_inc(spread_done, 16)
                if s.slot(A_LN2) == TILES - 1 and s.on(A_LN2):
                    sp.wait_ge(y_ready, s.count(A_LN2) + 1)
                    sp.sem_inc(waited_s, 1)
                    sp.dma_start(y_out[s.batch(A_LN2)].rearrange("(t p) d -> p t d", p=P), y[:, :, :]) \
                        .then_inc(y_out_done, 16)

            run(stage, sp)
            sp.wait_ge(y_out_done, BATCH * 16)

        @block.tensor
        def _(pe):
            def shifted_scores(s, c, j):
                k = GH * c + j
                if k == 0:
                    n, uses = s.turn(0)
                    pe.wait_ge(mrow_done[n], uses * 48)
                if some(seen := s.count(0, GH * TILES, k - 1)):
                    pe.wait_ge(p_ready, seen)
                pe.matmul(t_ps[:, k % 2, :], k_slot[0:QK_ROWS, s.g, j, P * c:P * c + P],
                          q_slot[0:QK_ROWS, s.g, j, :], start=True, stop=True).then_inc(t_full, 1)

            def score_pair(s, c, jj):
                k = 2 * c + jj
                if k == 0:
                    n, uses = s.turn(A_SMAX)
                    pe.wait_ge(gather_done[n], uses * 32)
                if some(seen := s.count(A_SMAX, 2 * TILES, k - 1)):
                    pe.wait_ge(s_read, seen)
                slot = s.slot(A_SMAX)
                for h in range(2):
                    mm = pe.matmul(s_ps[:, k % 2, h, :], q_slot[0:MAX_ROW, slot, 2 * jj + h, P * c:P * c + P],
                                   k_slot[0:MAX_ROW, slot, 2 * jj + h, :], start=True, stop=True)
                mm.then_inc(s_full, 1)

            def weighted_values(s, ahead, c):
                if c == 0:
                    pe.wait_ge(v_staged, s.count(ahead) + 1)
                    if some(seen := s.count(ahead)):
                        pe.wait_ge(o_read, seen)
                if some(seen := s.count(ahead, GH * TILES, GH * (c + 1))):
                    pe.wait_ge(p_ready, seen)
                for j in range(GH):
                    mm = pe.matmul(o_ps[32 * j:32 * j + 32, :], v_slot[:, s.slot(ahead), c, j, :],
                                   probs[:, c, j, :], start=(c == 0), stop=(c == TILES - 1))
                mm.then_inc(pv_done, 1)

            def phase_a(s):
                if s.on(A_WO):
                    pe.wait_ge(z1_ready, s.count(A_WO) + 1)
                if s.on(A_PREP - 1):
                    if some(seen := s.count(A_PREP - 1) + 1):
                        pe.wait_ge(v_read, seen)
                if s.on(A_FFN - 1):
                    if some(seen := s.count(A_FFN - 1) + 1):
                        pe.wait_ge(z2_ready, seen)
                if s.on(A_PREP):
                    pe.wait_ge(x_in_done, (s.batch(A_PREP) + 1) * 16)
                    mm = pe.transpose(m_ps[:, 0:P], x_in[:, s.slot(A_PREP), :], ident[:, :])
                if s.on(A_FFN):
                    n, uses = s.turn(A_FFN)
                    pe.wait_ge(x2_ready, s.count(A_FFN) + 1)
                    mm = pe.transpose(m_ps[:, P:2 * P], x2[:, n, :], ident[:, :])
                if s.on(A_MROW):
                    if some(seen := s.count(A_MROW, MSPLIT_STEPS, MSPLIT_STEPS)):
                        pe.wait_ge(msplit, seen)
                        pe.sem_inc(waited_t, 1)
                    mm = pe.transpose(max_t_ps, max_parts[:, :, :].rearrange("p a m -> p (a m)"), ident_b[:, :])
                mm.then_inc(a_full, 1)

            def phase_b(s):
                if isinstance(s.b, int) and s.count(A_PREP) == 0:
                    pe.wait_ge(wqkv_in, 3 * 16)
                pe.wait_ge(a_read, phase(s.b, s.g))
                if s.on(A_PREP):
                    pe.matmul(m_ps[:, 0:P], wq[:, :], x_t[:, 0, :], start=True, stop=True)
                    pe.matmul(m_ps[:, P:2 * P], wk[:, :], x_t[:, 0, :], start=True, stop=True)
                    mm = pe.matmul(m_ps[:, 2 * P:3 * P], x_t[:, 0, :], wv[:, :], start=True, stop=True)
                if s.on(A_FFN):
                    mm = pe.matmul(m_ps[:, 3 * P:4 * P], x_t[:, 1, :], wf[:, :], start=True, stop=True)
                mm.then_inc(b_full, 1)

            def phase_c(s):
                if s.on(A_PREP - 1):
                    if some(seen := s.count(A_PREP - 1) + 1):
                        pe.wait_ge(v_read, seen)
                if s.on(A_FFN - 1):
                    if some(seen := s.count(A_FFN - 1) + 1):
                        pe.wait_ge(z2_ready, seen)
                pe.wait_ge(att_ready, s.count(A_WO) + 1)
                pe.matmul(m_ps[:, 0:P], att_n[:, s.turn(A_WO)[0], :], wo[:, :], start=True, stop=True).then_inc(c_full, 1)

            pe.wait_ge(ident_done, 16)

            def stage(s):
                if isinstance(s.b, int) and s.count(A_SMAX) == 0:
                    pe.wait_ge(wf_wo_in, 2 * 16)
                    pe.wait_ge(setup_v, SETUP_V)
                    pe.wait_ge(setup_g, SETUP_G)
                for c in range(TILES):
                    for jj in range(2):
                        if s.on(0):
                            shifted_scores(s, c, 2 * jj)
                        if s.on(A_SMAX):
                            score_pair(s, c, jj)
                        if s.on(0):
                            shifted_scores(s, c, 2 * jj + 1)
                        if jj == 0:
                            if c == 0 and s.on(-1):
                                weighted_values(s, -1, TILES - 1)
                            if c > 0 and s.on(0):
                                weighted_values(s, 0, c - 1)
                    if c == 0 and s.on(A_WO):
                        phase_c(s)
                    if c == 1 and (s.on(A_PREP) or s.on(A_FFN) or s.on(A_MROW)):
                        phase_a(s)
                    if c == 2 and (s.on(A_PREP) or s.on(A_FFN)):
                        phase_b(s)

            run(stage, pe)

        @block.scalar
        def _(act):
            def exp(s, c, j):
                k = GH * c + j
                if some(seen := s.count(0, GH * TILES, k + 1)):
                    act.wait_ge(t_full, seen)
                if j == 0:
                    if some(seen := s.count(-1, TILES, c + 1)):
                        act.wait_ge(pv_done, seen)
                act.activation(probs[:, c, j, :], t_ps[:, k % 2, :], ACT.Exp, scale=SCALE).then_inc(p_ready, 1)

            def sums_out(s):
                if some(seen := s.count(-1, TILES, TILES)):
                    act.wait_ge(pv_done, seen)
                if s.on(-2):
                    n, uses = s.turn(-2)
                    act.wait_ge(o_out_done[n], uses * 16)
                act.copy(o_sum[:, :], o_ps[:, :]).then_inc(o_read, 1)

            def phase_a_out(s):
                act.wait_ge(a_full, phase(s.b, s.g))
                lo, hi = (0 if s.on(A_PREP) else 1), (2 if s.on(A_FFN) else 1)
                last = None
                if s.on(A_PREP) or s.on(A_FFN):
                    last = act.copy(x_t[:, lo:hi, :], m_ps[:, P * lo:P * hi].rearrange("p (a c) -> p a c", c=P))
                if s.on(A_MROW):
                    n, uses = s.turn(A_MROW - 1)
                    if s.on(A_MROW - 1):
                        act.wait_ge(mrow_done[n], uses * 48)
                    last = act.copy(max_t[:, :], max_t_ps)
                last.then_inc(a_read, 1)

            def phase_b_out(s):
                n, uses = s.turn(A_PREP)
                act.wait_ge(b_full, phase(s.b, s.g))
                if some(seen := s.count(A_PREP - 2, ROPE_STEPS, ROPE_STEPS)):
                    act.wait_ge(rope, seen)
                if s.on(A_PREP - 2):
                    m, uses = s.turn(A_PREP - 2)
                    act.wait_ge(swap_done[m], uses * 32)
                act.copy(qk_raw[:, n, :, :], m_ps[:, 0:2 * P].rearrange("p (a c) -> p a c", c=P)).then_inc(qk_read, 1)
                act.copy(v_nat[:, s.batch(A_PREP) & 3, s.slot(A_PREP), :], m_ps[:, 2 * P:3 * P]).then_inc(v_read, 1)

            def stage(s):
                for c in range(TILES):
                    for j in range(GH):
                        if s.on(0):
                            exp(s, c, j)
                        if c == 0 and j == 1 and s.on(-1):
                            sums_out(s)
                        if c == 2 and j == 1 and (s.on(A_PREP) or s.on(A_FFN) or s.on(A_MROW)):
                            phase_a_out(s)
                        if c == 3 and j == 1 and s.on(A_PREP):
                            phase_b_out(s)

            run(stage, act)

        @block.vector
        def _(dve):
            def signs():
                dve.wait_ge(wf_wo_in, 2 * 16)
                dve.tensor_scalar(wf_pos[:, :], wf_raw[:, :], 0.0, None, ALU.is_gt)
                dve.tensor_scalar(wf_neg[:, :], wf_raw[:, :], 0.0, None, ALU.is_lt).then_inc(setup_v, 1)
                dve.wait_ge(setup_v, 1)
                dve.tensor_tensor(wf[:, :], wf_pos[:, :], wf_neg[:, :], ALU.subtract).then_inc(setup_v, 1)

            def pair_max(s, k):
                c, jj = k // 2, k % 2
                if k == 0:
                    if some(seen := s.count(A_SMAX - 2, MSPLIT_STEPS, MSPLIT_STEPS)):
                        dve.wait_ge(msplit, seen)
                if some(seen := s.count(A_SMAX, 2 * TILES, k + 1)):
                    dve.wait_ge(s_full, seen)
                dve.tensor_reduce(neg_max[:, s.turn(A_SMAX)[0], 2 * jj:2 * jj + 2, c], s_ps[:, k % 2, :, :],
                                  AX.X, ALU.max, negate=True).then_inc(s_read, 1)

            def add_first(s, ahead):
                dve.wait_ge(c_full, s.count(ahead) + 1)
                dve.wait_ge(x_res_done, (s.batch(ahead) + 1) * 16)
                if some(seen := s.count(ahead - 1) + 1):
                    dve.wait_ge(x2_ready, seen)
                dve.tensor_tensor(z1[:, :], m_ps[:, 0:P], x_res[:, s.slot(ahead), :], ALU.add).then_inc(z1_ready, 1)

            def add_second(s, ahead):
                n, uses = s.turn(ahead)
                dve.wait_ge(b_full, phase(s.b, s.g))
                if s.on(A_PREP):
                    dve.wait_ge(v_read, s.count(A_PREP) + 1)
                if some(seen := s.count(ahead - 1) + 1):
                    dve.wait_ge(y_ready, seen)
                dve.tensor_tensor(z2[:, :], m_ps[:, 3 * P:4 * P], x2[:, n, :], ALU.add).then_inc(z2_ready, 1)

            def stats(s, ahead, z, st, ready, done):
                dve.wait_ge(ready, s.count(ahead) + 1)
                dve.bn_stats(st[:, :], z[:, :]).then_inc(done, 1)

            def moments(s, ahead, st, mv, ready, done):
                dve.wait_ge(ready, s.count(ahead) + 1)
                dve.sem_inc(waited_v, 1)
                dve.bn_aggr(mv[:, :], st[:, :]).then_inc(done, 1)

            def factors(s, ahead, mv, nr, ready, done):
                dve.wait_ge(ready, s.count(ahead) + 1)
                dve.tensor_scalar(nr[:, 0:1], mv[:, 0:1], -1.0, None, ALU.mult)
                dve.tensor_scalar(nr[:, 1:2], mv[:, 1:2], EPS, None, ALU.add).then_inc(done, 1)

            def reciprocals(s):
                dve.wait_ge(att_in_done, (s.batch(A_DIVIDE) + 1) * (GH * 16))
                if some(seen := s.count(A_DIVIDE)):
                    dve.wait_ge(att_ready, seen)
                t = s.slot(A_DIVIDE)
                dve.reciprocal(att_rcp[:, :], att[:, 1, P * t:P * t + P]).then_inc(rcp_ready, 1)

            def stage(s):
                if isinstance(s.b, int) and s.count(A_ROPE) == TILES:
                    signs()
                if s.on(A_ROPE) and not s.on(A_ROPE - TILES):
                    if s.count(A_ROPE) == 0:
                        dve.wait_ge(table_in, 16)
                    rotate(dve, waited_v, s)
                    split_rotated(dve, waited_v, s)
                for k in range(2 * TILES):
                    if s.on(A_SMAX):
                        pair_max(s, k)
                    if k == 0 and s.on(A_DIVIDE):
                        reciprocals(s)
                    if k == 1 and s.on(A_WO):
                        add_first(s, A_WO)
                    if k == 0 and s.on(A_LN2):
                        stats(s, A_LN2, z2, st2, z2_ready, st2_ready)
                    if k == 1 and s.on(A_LN2):
                        moments(s, A_LN2, st2, mv2, st2_ready, mv2_ready)
                    if k == 2 and s.on(A_LN2):
                        factors(s, A_LN2, mv2, nr2, mv2_ready, ln2_ready)
                    if k == 3 and s.on(A_WO):
                        stats(s, A_WO, z1, st1, z1_ready, st1_ready)
                    if k == 4 and s.on(A_WO):
                        moments(s, A_WO, st1, mv1, st1_ready, mv1_ready)
                        factors(s, A_WO, mv1, nr1, mv1_ready, ln1_ready)
                    if k == 7 and s.on(A_FFN):
                        add_second(s, A_FFN)

            run(stage, dve)

        @block.gpsimd
        def _(pool):
            ones2 = float(np.array([0x3F803F80], np.uint32).view(np.float32)[0])
            pool.memset(k_slot[:, :, :, :].bitcast(fp32), 0.0).then_inc(setup_g, 1)
            pool.memset(q_slot[:, :, :, :].bitcast(fp32), 0.0).then_inc(setup_g, 1)
            pool.wait_ge(setup_g, 2)
            pool.memset(k_slot[MAX_ROW:QK_ROWS, :, :, :].bitcast(fp32), ones2).then_inc(setup_g, 1)
            pool.wait_ge(setup_g, 3)
            pool.memset(minus_half[:, :], -0.5).then_inc(setup_g, 1)
            pool.memset(v_slot[:, :, :, :, HD:2 * HD], 1.0).then_inc(setup_g, 1)
            pool.memset(v_slot[:, :, :, :, 2 * HD:32], 0.0).then_inc(setup_g, 1)
            pool.wait_ge(setup_g, 6)
            pool.wait_ge(ident_done, 16)
            pool.tensor_copy(ident_b[:, :], ident[:, :]).then_inc(setup_g, 2)
            pool.wait_ge(table_in, 16)

            def split_maxima(s):
                n, _ = s.turn(A_MROW)
                m = neg_max[:, n, :, :].rearrange("p j t -> p (j t)")
                at = lambda k: s.count(A_MROW, MSPLIT_STEPS, k)
                if some(seen := s.count(A_MROW, 2 * TILES, 2 * TILES)):
                    pool.wait_ge(s_read, seen)
                    pool.sem_inc(waited_g, 1)
                if some(seen := phase(s.b, s.g) - 1):
                    pool.wait_ge(a_full, seen)
                    pool.sem_inc(waited_g, 1)
                pool.tensor_copy(max_parts[:, 0, :], m).then_inc(msplit, 1)
                if some(seen := at(1)):
                    pool.wait_ge(msplit, seen)
                    pool.sem_inc(waited_g, 1)
                pool.tensor_tensor(max_rest[:, :], m, max_parts[:, 0, :], ALU.subtract).then_inc(msplit, 1)
                if some(seen := at(2)):
                    pool.wait_ge(msplit, seen)
                    pool.sem_inc(waited_g, 1)
                pool.tensor_copy(max_parts[:, 1, :], max_rest[:, :]).then_inc(msplit, 1)
                if some(seen := at(3)):
                    pool.wait_ge(msplit, seen)
                    pool.sem_inc(waited_g, 1)
                pool.tensor_tensor(max_parts[:, 2, :], max_rest[:, :], max_parts[:, 1, :], ALU.subtract).then_inc(msplit, 1)

            def stage_values(s):
                g = s.slot(A_MROW)
                b2 = s.batch(A_MROW)
                pool.wait_ge(v_read, (b2 + 1) * TILES)
                pool.sem_inc(waited_g, 1)
                if some(seen := s.count(A_MROW - GROUPS, TILES, TILES)):
                    pool.wait_ge(pv_done, seen)
                    pool.sem_inc(waited_g, 1)
                pool.tensor_copy(v_slot[:, g, :, :, 0:HD],
                                 v_nat[:, b2 & 3, :, 32 * g:32 * g + 32].rearrange("p t (j d) -> p t j d", d=HD)) \
                    .then_inc(v_staged, 1)

            def normalise(s, ahead, z, nr, rstd, out, ready, powered, done):
                pool.wait_ge(ready, s.count(ahead) + 1)
                pool.sem_inc(waited_g, 1)
                pool.tensor_tensor(rstd[:, :], nr[:, 1:2], minus_half[:, :], ALU.pow).then_inc(powered, 1)
                pool.wait_ge(powered, s.count(ahead) + 1)
                pool.sem_inc(waited_g, 1)
                pool.tensor_scalar(out, z[:, :], nr[:, 0:1], rstd[:, :], ALU.add, ALU.mult).then_inc(done, 1)

            def divide(s, ahead):
                t = s.slot(ahead)
                pool.wait_ge(rcp_ready, s.count(ahead) + 1)
                pool.sem_inc(waited_g, 1)
                if some(seen := s.count(ahead - 1)):
                    pool.wait_ge(c_full, seen)
                    pool.sem_inc(waited_g, 1)
                pool.tensor_tensor(att_n[:, s.turn(ahead)[0], :], att[:, 0, P * t:P * t + P], att_rcp[:, :], ALU.mult) \
                    .then_inc(att_ready, 1)

            def stage(s):
                if s.on(A_MROW):
                    split_maxima(s)
                if s.on(A_DIVIDE):
                    divide(s, A_DIVIDE)
                if s.on(A_ROPE) and s.on(A_ROPE - TILES):
                    if isinstance(s.b, int) and s.count(A_ROPE) == TILES:
                        pool.wait_ge(rope, TILES * ROPE_STEPS)
                    rotate(pool, waited_g, s)
                    split_rotated(pool, waited_g, s)
                if s.on(A_LN2):
                    if s.slot(A_LN2) == 0:
                        if some(seen := s.batch(A_LN2) * 16):
                            pool.wait_ge(y_out_done, seen)
                            pool.sem_inc(waited_g, 1)
                    normalise(s, A_LN2, z2, nr2, rstd2, y[:, s.slot(A_LN2), :], ln2_ready, pow2_ready, y_ready)
                if s.on(A_MROW):
                    stage_values(s)
                if s.on(A_WO):
                    if some(seen := s.count(A_WO - 2) + 1):
                        pool.wait_ge(z2_ready, seen)
                        pool.sem_inc(waited_g, 1)
                    normalise(s, A_WO, z1, nr1, rstd1, x2[:, s.turn(A_WO)[0], :], ln1_ready, pow1_ready, x2_ready)

            run(stage, pool)


def rope_table():
    import numpy as np
    inv = (np.float32(1.0) / np.power(np.float32(10000.0), np.arange(0, HD, 2, dtype=np.float32) / np.float32(HD))).astype(np.float32)
    ang = (np.arange(SEQ, dtype=np.float32)[None, :] * inv[:, None]).astype(np.float32)
    cos, sin = np.cos(ang).astype(np.float32), np.sin(ang).astype(np.float32)
    tab = np.zeros((2, HD // 2, HEADS, 2, SEQ), np.float32)
    tab[:, :, :, 0, :] = cos[None, :, None, :]
    tab[0, :, :, 1, :] = -sin[:, None, :]
    tab[1, :, :, 1, :] = sin[:, None, :]
    return tab.reshape(P, 2, SEQ)


def kernel(**inputs):
    import numpy as np
    import concourse.bacc as bacc
    from concourse.bass_utils import run_bass_kernel_spmd

    def rows_of_qk(w):
        w = w.reshape(GROUPS, GH, HD // 2, 2, D).transpose(3, 2, 1, 0, 4).reshape(D, D)
        return np.ascontiguousarray(w.T)

    a = {k: np.asarray(v) for k, v in inputs.items()}
    wo_rows = a["L0_attn_wo"].T.reshape(GROUPS, GH, HD, D).transpose(1, 2, 0, 3).reshape(D, D)
    arrays = {
        "x": np.ascontiguousarray(a["L0_attn_x"]),
        "wq_t": rows_of_qk(a["L0_attn_wq"]),
        "wk_t": rows_of_qk(a["L0_attn_wk"]),
        "wv_t": np.ascontiguousarray(a["L0_attn_wv"].T),
        "wo_t": np.ascontiguousarray(wo_rows),
        "wf_t": np.ascontiguousarray(a["L0_ffn_weight"].T),
        "rope_tab": rope_table(),
        "ident_in": np.eye(P, dtype=np.float32),
    }
    nc = bacc.Bacc("TRN2", target_bir_lowering=False, num_devices=1)
    args = [nc.dram_tensor(k, v.shape, mybir.dt.from_np(v.dtype), kind="ExternalInput").ap() for k, v in arrays.items()]
    out = nc.dram_tensor("y_out", (BATCH, SEQ, D), mybir.dt.float32, kind="ExternalOutput").ap()
    body(nc, *args, out)
    r = run_bass_kernel_spmd(nc, [arrays], core_ids=[0])
    return r.results[0]["y_out"]
```

```python
from contextlib import ExitStack

import concourse.bass as bass
import numpy as np
from concourse import mybir
from concourse.alu_op_type import AluOpType as ALU

BATCH, SEQ, D = 16, 512, 128
HEADS = 16
HD = D // HEADS
P = 128
TILES = SEQ // P
GROUPS = 4
GH = HEADS // GROUPS
STAGES = BATCH * GROUPS
EPS = 1e-5
SCALE = HD ** -0.5
BATCH_DENS = HEADS * SEQ // P

TERMS_Q = [0, 1, 2, 0, 1, 0]
TERMS_K = [0, 0, 0, 1, 1, 2]
TERM_ROWS = len(TERMS_Q) * HD
MAX_ROW = 96
QK_ROWS = MAX_ROW + 3

A_PREP = 9
A_ROPE = 8
A_GATHER = 3
A_SMAX = 2
A_MROW = 1
A_RCP = -5
A_DIVIDE = -6
A_WO = -7
A_FFN = -8
A_LN2 = -9

LAST_DIVIDES = (STAGES + 3, STAGES + 4)


class Step:

    def __init__(self, b, g):
        self.b, self.g = b, g

    def on(self, ahead):
        if not isinstance(self.b, int):
            return True
        first = TILES if ahead >= A_ROPE else 0
        end = STAGES if ahead > -GROUPS else STAGES - TILES
        return first <= GROUPS * self.b + self.g + ahead < end

    def slot(self, ahead):
        return (self.g + ahead) % GROUPS

    def batch(self, ahead):
        return self.b + (self.g + ahead) // GROUPS

    def count(self, ahead, per=1, more=0):
        return self.b * (GROUPS * per) + ((self.g + ahead) * per + more)

    def turn(self, ahead):
        i = self.g + ahead
        return i % 2, self.b * (GROUPS // 2) + (i // 2 + 1)


def some(value):
    return not isinstance(value, int) or value > 0


def body(nc, x, x_t, wq_t, wk_t, wv_t, wo_t, wf_t, rope_tab, ident_in, y_out):
    fp32, bf16 = mybir.dt.float32, mybir.dt.bfloat16
    ACT = mybir.ActivationFunctionType
    AX = mybir.AxisListType

    qk_scr = nc.dram_tensor("qk_scr", (2, 2, len(TERMS_Q), HD, GH, GROUPS, SEQ), bf16, kind="Internal").ap()
    o_scr = nc.dram_tensor("o_scr", (2, P, GROUPS, SEQ), fp32, kind="Internal").ap()
    rcp_scr = nc.dram_tensor("rcp_scr", (GH, 1, GROUPS * SEQ), fp32, kind="Internal").ap()

    with ExitStack() as ctx:
        def sb(name, shape, dt=fp32):
            return ctx.enter_context(nc.sbuf_tensor(name, shape, dt))

        def ps(name, shape):
            return ctx.enter_context(nc.psum_tensor(name, shape, fp32))

        def sem(name):
            return ctx.enter_context(nc.semaphore(name))

        wq = sb("wq", [P, D])
        wk = sb("wk", [P, D])
        wv = sb("wv", [P, D])
        wo = sb("wo", [P, D])
        wf_raw = sb("wf_raw", [P, D])
        wf_pos = sb("wf_pos", [P, D])
        wf_neg = sb("wf_neg", [P, D])
        wf = sb("wf", [P, D])
        cos_sin = sb("cos_sin", [P, 2, SEQ])
        ident = sb("ident", [P, P])
        ident_b = sb("ident_b", [P, P], bf16)

        x_in = sb("x_in", [P, SEQ])
        qk_raw = sb("qk_raw", [P, 2, 2, P])
        qk_swap = sb("qk_swap", [P, 2, 2, P])
        rope_a = sb("rope_a", [P, 2, P])
        rope_b = sb("rope_b", [P, 2, P])
        rope_r = sb("rope_r", [P, 2, P])
        rope_rest = sb("rope_rest", [P, 2, P])
        parts = sb("parts", [P, 2, 2, 3, SEQ], bf16)
        v_nat = sb("v_nat", [P, 4, TILES, D])

        q_slot = sb("q_slot", [P, GROUPS, GH, SEQ], bf16)
        k_slot = sb("k_slot", [P, GROUPS, GH, SEQ], bf16)
        v_slot = sb("v_slot", [P, GROUPS, TILES, GH, 32])
        neg_max = sb("neg_max", [P, 2, GH, TILES])
        max_rest = sb("max_rest", [P, GH * TILES])
        max_parts = sb("max_parts", [P, 3, GH * TILES], bf16)
        max_t = sb("max_t", [3 * GH * TILES, P], bf16)
        probs = sb("probs", [P, TILES, GH, SEQ])
        o_sum = sb("o_sum", [P, SEQ])

        den = sb("den", [P, BATCH_DENS])
        den_rcp = sb("den_rcp", [P, BATCH_DENS])
        att = sb("att", [P, 2, SEQ])
        att_n = sb("att_n", [P, 2, P])
        x_res = sb("x_res", [P, TILES, D])
        z1 = sb("z1", [P, D])
        st1 = sb("st1", [P, 6])
        mv1 = sb("mv1", [P, 2])
        nr1 = sb("nr1", [P, 2])
        rstd1 = sb("rstd1", [P, 1])
        x2 = sb("x2", [P, 2, D])
        x2_t = sb("x2_t", [P, P])
        z2 = sb("z2", [P, D])
        st2 = sb("st2", [P, 6])
        mv2 = sb("mv2", [P, 2])
        nr2 = sb("nr2", [P, 2])
        rstd2 = sb("rstd2", [P, 1])
        minus_half = sb("minus_half", [P, TILES])
        y = sb("y", [P, TILES, D])

        first_a = sb("first_a", [P, SEQ])
        first_b = sb("first_b", [P, SEQ])
        first_r = sb("first_r", [P, SEQ])
        first_rest = sb("first_rest", [P, SEQ])

        last_att = sb("last_att", [P, 2, SEQ])
        last_x = sb("last_x", [P, TILES, D])
        last_att_n = sb("last_att_n", [P, SEQ])
        last_z = sb("last_z", [P, TILES, D])
        last_st = sb("last_st", [P, TILES, 6])
        last_mv = sb("last_mv", [P, TILES, 2])
        last_nr = sb("last_nr", [P, 2, TILES])
        last_rstd = sb("last_rstd", [P, TILES])
        last_x2 = sb("last_x2", [P, TILES, D])
        last_x2_t = sb("last_x2_t", [P, SEQ])

        s_ps = ps("s_ps", [P, 2, 2, SEQ])
        t_ps = ps("t_ps", [P, 2, SEQ])
        o_ps = ps("o_ps", [P, SEQ])
        m_ps = ps("m_ps", [P, SEQ])
        max_t_ps = m_ps[0:3 * GH * TILES, 2 * P:2 * P + P // 2].bitcast(bf16)

        ident_done = sem("ident_done")
        w_in = [sem(f"w{n}_in") for n in "qkv"]
        table_in = sem("table_in")
        wf_wo_in = sem("wf_wo_in")
        x_in_done = sem("x_in_done")
        x_res_done = sem("x_res_done")
        swap_done = [sem(f"swap_done{n}") for n in range(2)]
        spread_done = sem("spread_done")
        gather_done = [sem(f"gather_done{n}") for n in range(2)]
        mrow_done = [sem(f"mrow_done{n}") for n in range(2)]
        o_out_done = [sem(f"o_out_done{n}") for n in range(2)]
        den_in_done = sem("den_in_done")
        rcp_out_done = sem("rcp_out_done")
        att_in_done = sem("att_in_done")
        y_out_done = sem("y_out_done")

        a_full = sem("a_full")
        b_full = sem("b_full")
        c_full = sem("c_full")
        d_full = sem("d_full")
        s_full = sem("s_full")
        t_full = sem("t_full")
        pv_done = sem("pv_done")

        a_read = sem("a_read")
        qk_read = sem("qk_read")
        v_read = sem("v_read")
        p_ready = sem("p_ready")

        setup_v = sem("setup_v")
        s_read = sem("s_read")
        o_read = sem("o_read")
        z1_ready = sem("z1_ready")
        st1_ready = sem("st1_ready")
        mv1_ready = sem("mv1_ready")
        ln1_ready = sem("ln1_ready")
        z2_ready = sem("z2_ready")
        st2_ready = sem("st2_ready")
        mv2_ready = sem("mv2_ready")
        ln2_ready = sem("ln2_ready")
        rcp_ready = sem("rcp_ready")

        setup_g = sem("setup_g")
        msplit = sem("msplit")
        rope = sem("rope")
        v_staged = sem("v_staged")
        pow1_ready = sem("pow1_ready")
        pow2_ready = sem("pow2_ready")
        x2_ready = sem("x2_ready")
        att_ready = sem("att_ready")
        y_ready = sem("y_ready")

        first_full = sem("first_full")
        first_v_full = sem("first_v_full")
        first_rope = sem("first_rope")

        last_x_done = sem("last_x_done")
        last_in_done = [sem(f"last_in_done{n}") for n in range(2)]
        last_wo_full = sem("last_wo_full")
        last_x2_t_full = sem("last_x2_t_full")
        last_ffn_full = sem("last_ffn_full")
        last_x2_t_ready = sem("last_x2_t_ready")
        last_rcp_ready = sem("last_rcp_ready")
        last_z_ready = sem("last_z_ready")
        last_st_ready = sem("last_st_ready")
        last_mv_ready = sem("last_mv_ready")
        last_nr_ready = sem("last_nr_ready")
        last_out_ready = sem("last_out_ready")
        last_att_ready = sem("last_att_ready")
        last_rstd_ready = sem("last_rstd_ready")

        waited_s, waited_t, waited_v, waited_g = (sem(f"waited_{n}") for n in "stvg")

        ROPE_STEPS, MSPLIT_STEPS = 7, 4
        FIRST_STEPS = 7
        SETUP_G, SETUP_V = 7, 2
        SPREAD = 6 * 16

        def phase(b, g):
            return b * GROUPS + (g + A_MROW + 1)

        def tile(t):
            return slice(P * t, P * t + P)

        def run(stage, eng):
            first, last = 3, BATCH - 2 - A_PREP // GROUPS
            for b in range(-A_PREP // GROUPS, first):
                for g in range(GROUPS):
                    stage(Step(b, g))
            with eng.Fori(first, last + 1) as b:
                for g in range(GROUPS):
                    stage(Step(b, g))
            for b in range(last + 1, BATCH + 2):
                for g in range(GROUPS):
                    stage(Step(b, g))

        block = ctx.enter_context(nc.Block())

        @block.sync
        def _(sp):
            def load_batch(buf, done, b):
                sp.dma_start(buf[:, :, :], x[b].rearrange("(t p) d -> p t d", p=P)).then_inc(done, 16)

            def load_transposed(b):
                sp.dma_start(x_in[:, :], x_t[b]).then_inc(x_in_done, 16)

            def spread(b2, side):
                terms = (TERMS_Q, TERMS_K)[side]
                for at, k in ((0, 3), (3, 2), (5, 1)):
                    first = terms[at]
                    if terms[at:at + k] == list(range(first, first + k)):
                        src = parts[:, b2 & 1, side, first:first + k, :]
                    else:
                        src = parts[:, b2 & 1, side, first:first + 1, :].to_broadcast([P, k, SEQ])
                    sp.dma_start(qk_scr[b2 & 1, side, at:at + k].rearrange("t r j g c -> (r j g) t c"), src) \
                        .then_inc(spread_done, 16)

            load_transposed(0)
            sp.dma_start(wq[:, :], wq_t).then_inc(w_in[0], 16)
            sp.dma_start(cos_sin[:, :, :], rope_tab).then_inc(table_in, 16)
            sp.dma_start(wk[:, :], wk_t).then_inc(w_in[1], 16)
            sp.dma_start(wv[:, :], wv_t).then_inc(w_in[2], 16)
            sp.dma_start(ident[:, :], ident_in).then_inc(ident_done, 16)
            for dst, src in ((wf_raw, wf_t), (wo, wo_t)):
                sp.dma_start(dst[:, :], src).then_inc(wf_wo_in, 16)

            for n in range(2):
                sp.sem_inc(swap_done[n], TILES // 2 * 32)
            sp.sem_inc(qk_read, TILES)
            sp.sem_inc(rope, TILES * ROPE_STEPS)
            sp.wait_ge(first_v_full, 1)
            load_transposed(1)
            for side in range(2):
                sp.wait_ge(first_rope, (side + 1) * 2 * FIRST_STEPS)
                spread(0, side)

            def stage(s):
                if s.on(A_GATHER):
                    n, uses = s.turn(A_GATHER)
                    par, g = s.batch(A_GATHER) & 1, s.slot(A_GATHER)
                    if isinstance(s.b, int) and s.count(A_GATHER) == 0:
                        sp.wait_ge(setup_g, SETUP_G)
                    sp.wait_ge(spread_done, (s.batch(A_GATHER) + 1) * SPREAD)
                    sp.sem_inc(waited_s, 1)
                    if some(seen := s.count(A_GATHER - GROUPS + 1, GH * TILES)):
                        sp.wait_ge(t_full, seen)
                        sp.sem_inc(waited_s, 1)
                    for side, slot in ((0, q_slot), (1, k_slot)):
                        sp.dma_start(slot[0:TERM_ROWS, g, :, :],
                                     qk_scr[par, side, :, :, :, g, :].rearrange("t r j c -> (t r) j c")) \
                            .then_inc(gather_done[n], 16)
                if s.on(-1):
                    n, uses = s.turn(-1)
                    if some(seen := s.count(-1) + 1):
                        sp.wait_ge(o_read, seen)
                        sp.sem_inc(waited_s, 1)
                    sp.dma_start(o_scr[s.batch(-1) & 1, :, s.slot(-1), :], o_sum[:, :]).then_inc(o_out_done[n], 16)
                if s.slot(A_RCP) == 0 and s.on(A_RCP):
                    sp.wait_ge(rcp_ready, s.batch(A_RCP) + 1)
                    sp.sem_inc(waited_s, 1)
                    if some(seen := s.batch(A_RCP) * ((GH + 1) * 16)):
                        sp.wait_ge(att_in_done, seen)
                        sp.sem_inc(waited_s, 1)
                    sp.dma_start(rcp_scr.rearrange("j a (q e) -> (j a q) e", e=BATCH_DENS), den_rcp[:, :]) \
                        .then_inc(rcp_out_done, 16)
                if s.on(A_MROW):
                    n, uses = s.turn(A_MROW)
                    sp.wait_ge(a_read, phase(s.b, s.g))
                    sp.sem_inc(waited_s, 1)
                    for part in range(3):
                        sp.dma_start(
                            q_slot[MAX_ROW + part:MAX_ROW + part + 1, s.slot(A_MROW), :, :]
                            .rearrange("p j (t c) -> p (j t) c", t=TILES),
                            max_t[part * GH * TILES:(part + 1) * GH * TILES, :],
                        ).then_inc(mrow_done[n], 16)
                if s.g == 0 and s.on(-GROUPS):
                    b2 = s.batch(-GROUPS)
                    for n in range(2):
                        if some(seen := s.turn(-2 + n)[1] * 16):
                            sp.wait_ge(o_out_done[n], seen)
                            sp.sem_inc(waited_s, 1)
                    if some(seen := b2):
                        sp.wait_ge(rcp_ready, seen)
                        sp.sem_inc(waited_s, 1)
                    sp.dma_start(
                        den[:, :],
                        o_scr[b2 & 1, :, :, :].rearrange("(j r) g c -> j r (g c)", r=32)[:, HD, :]
                        .rearrange("j (q e) -> j q e", e=BATCH_DENS),
                    ).then_inc(den_in_done, 16)
                if s.slot(A_RCP) == 0 and s.on(A_RCP):
                    b2 = s.batch(A_RCP)
                    if some(seen := s.count(A_DIVIDE) + 1):
                        sp.wait_ge(att_ready, seen)
                        sp.sem_inc(waited_s, 1)
                    sp.dma_start(
                        att[:, 0, :],
                        o_scr[b2 & 1, :, :, :].rearrange("(j r) g c -> j r g c", r=32)[:, 0:HD, :, :]
                        .rearrange("j d g c -> j (d g) c"),
                    ).then_inc(att_in_done, 16)
                    sp.wait_ge(rcp_out_done, (b2 + 1) * 16)
                    sp.sem_inc(waited_s, 1)
                    for j in range(GH):
                        sp.dma_start(
                            att[32 * j:32 * j + 32, 1, :],
                            rcp_scr[j].to_broadcast([HD, GROUPS * SEQ]).rearrange("d (g c) -> d g c", g=GROUPS),
                        ).then_inc(att_in_done, 16)
                if s.slot(A_WO) == TILES - 1 and s.on(A_WO + 1):
                    if some(seen := s.count(A_WO) + 1):
                        sp.wait_ge(z1_ready, seen)
                        sp.sem_inc(waited_s, 1)
                    load_batch(x_res, x_res_done, s.batch(A_WO + 1))
                if isinstance(s.b, int) and s.count(0) == STAGES - TILES:
                    load_batch(last_x, last_x_done, BATCH - 1)
                if s.slot(A_PREP) == TILES - 1 and s.on(A_PREP) and s.on(A_PREP + 1):
                    sp.wait_ge(b_full, s.count(A_PREP, 1, 1 - TILES))
                    sp.sem_inc(waited_s, 1)
                    load_transposed(s.batch(A_PREP + 1))
                if s.on(A_PREP):
                    n, uses = s.turn(A_PREP)
                    sp.wait_ge(qk_read, s.count(A_PREP) + 1)
                    sp.sem_inc(waited_s, 1)
                    for half in range(2):
                        sp.dma_start(qk_swap[64 * half:64 * half + 64, n, :, :],
                                     qk_raw[64 - 64 * half:128 - 64 * half, n, :, :]).then_inc(swap_done[n], 16)
                if s.slot(A_ROPE) == TILES - 1 and s.on(A_ROPE):
                    b2 = s.batch(A_ROPE)
                    sp.wait_ge(rope, (b2 + 1) * (GROUPS * ROPE_STEPS))
                    sp.sem_inc(waited_s, 1)
                    for n in range(2):
                        if some(seen := (b2 - 1) * 64):
                            sp.wait_ge(gather_done[n], seen)
                            sp.sem_inc(waited_s, 1)
                    for side in range(2):
                        spread(b2, side)
                if s.slot(A_LN2) == TILES - 1 and s.on(A_LN2):
                    sp.wait_ge(y_ready, s.count(A_LN2) + 1)
                    sp.sem_inc(waited_s, 1)
                    sp.dma_start(y_out[s.batch(A_LN2)].rearrange("(t p) d -> p t d", p=P), y[:, :, :]) \
                        .then_inc(y_out_done, 16)
                if isinstance(s.b, int) and s.count(-1) == STAGES - 1:
                    par = (BATCH - 1) & 1
                    for n in range(2):
                        sp.wait_ge(o_out_done[n], STAGES // 2 * 16)
                    for j in range(GH):
                        sp.dma_start(
                            last_att[32 * j:32 * j + 32, 1, :],
                            o_scr[par, 32 * j + HD:32 * j + HD + 1, :, :].to_broadcast([HD, GROUPS, SEQ]),
                        ).then_inc(last_in_done[1], 16)
                    sp.dma_start(
                        last_att[:, 0, :],
                        o_scr[par, :, :, :].rearrange("(j r) g c -> j r g c", r=32)[:, 0:HD, :, :]
                        .rearrange("j d g c -> j (d g) c"),
                    ).then_inc(last_in_done[0], 16)

            run(stage, sp)
            for half in range(2):
                ts = slice(2 * half, 2 * half + 2)
                sp.wait_ge(last_out_ready, TILES + 2 * half + 2)
                sp.dma_start(y_out[BATCH - 1].rearrange("(t p) d -> p t d", p=P)[:, ts, :], y[:, ts, :]) \
                    .then_inc(y_out_done, 16)
            sp.wait_ge(y_out_done, (BATCH + 1) * 16)

        @block.tensor
        def _(pe):
            def shifted_scores(s, c, j):
                k = GH * c + j
                if k == 0:
                    n, uses = s.turn(0)
                    pe.wait_ge(mrow_done[n], uses * 48)
                if some(seen := s.count(0, GH * TILES, k - 1)):
                    pe.wait_ge(p_ready, seen)
                pe.matmul(t_ps[:, k % 2, :], k_slot[0:QK_ROWS, s.g, j, P * c:P * c + P],
                          q_slot[0:QK_ROWS, s.g, j, :], start=True, stop=True).then_inc(t_full, 1)

            def score_pair(s, c, jj):
                k = 2 * c + jj
                if k == 0:
                    n, uses = s.turn(A_SMAX)
                    pe.wait_ge(gather_done[n], uses * 32)
                if some(seen := s.count(A_SMAX, 2 * TILES, k - 1)):
                    pe.wait_ge(s_read, seen)
                slot = s.slot(A_SMAX)
                for h in range(2):
                    mm = pe.matmul(s_ps[:, k % 2, h, :], q_slot[0:MAX_ROW, slot, 2 * jj + h, P * c:P * c + P],
                                   k_slot[0:MAX_ROW, slot, 2 * jj + h, :], start=True, stop=True)
                mm.then_inc(s_full, 1)

            def weighted_values(s, ahead, c):
                if c == 0:
                    pe.wait_ge(v_staged, s.count(ahead) + 1)
                    if some(seen := s.count(ahead)):
                        pe.wait_ge(o_read, seen)
                if some(seen := s.count(ahead, GH * TILES, GH * (c + 1))):
                    pe.wait_ge(p_ready, seen)
                for j in range(GH):
                    mm = pe.matmul(o_ps[32 * j:32 * j + 32, :], v_slot[:, s.slot(ahead), c, j, :],
                                   probs[:, c, j, :], start=(c == 0), stop=(c == TILES - 1))
                mm.then_inc(pv_done, 1)

            def phase_c(s):
                if s.on(A_PREP - 1):
                    if some(seen := s.count(A_PREP - 1) + 1):
                        pe.wait_ge(v_read, seen)
                if s.on(A_FFN - 1):
                    if some(seen := s.count(A_FFN - 1) + 1):
                        pe.wait_ge(z2_ready, seen)
                pe.wait_ge(att_ready, s.count(A_WO) + 1)
                pe.matmul(m_ps[:, 0:P], att_n[:, s.turn(A_WO)[0], :], wo[:, :], start=True, stop=True).then_inc(c_full, 1)

            def phase_a(s):
                if s.on(A_WO):
                    pe.wait_ge(z1_ready, s.count(A_WO) + 1)
                if s.on(A_PREP - 1):
                    if some(seen := s.count(A_PREP - 1) + 1):
                        pe.wait_ge(v_read, seen)
                if s.on(A_FFN - 1):
                    if some(seen := s.count(A_FFN - 1) + 1):
                        pe.wait_ge(z2_ready, seen)
                if s.on(A_FFN):
                    n, uses = s.turn(A_FFN)
                    pe.wait_ge(x2_ready, s.count(A_FFN) + 1)
                    mm = pe.transpose(m_ps[:, P:2 * P], x2[:, n, :], ident[:, :])
                if s.on(A_MROW):
                    if some(seen := s.count(A_MROW, MSPLIT_STEPS, MSPLIT_STEPS)):
                        pe.wait_ge(msplit, seen)
                        pe.sem_inc(waited_t, 1)
                    mm = pe.transpose(max_t_ps, max_parts[:, :, :].rearrange("p a m -> p (a m)"), ident_b[:, :])
                mm.then_inc(a_full, 1)

            def phase_b(s):
                x_tile = x_in[:, tile(s.slot(A_PREP))]
                if s.on(A_MROW) or s.on(A_FFN):
                    pe.wait_ge(a_read, phase(s.b, s.g))
                elif s.on(A_PREP - 1):
                    pe.wait_ge(v_read, s.count(A_PREP - 1) + 1)
                pe.wait_ge(x_in_done, (s.batch(A_PREP) + 1) * 16)
                pe.matmul(m_ps[:, 0:P], wq[:, :], x_tile, start=True, stop=True)
                pe.matmul(m_ps[:, P:2 * P], wk[:, :], x_tile, start=True, stop=True)
                pe.matmul(m_ps[:, 2 * P:3 * P], x_tile, wv[:, :], start=True, stop=True).then_inc(b_full, 1)

            def phase_d(s):
                pe.wait_ge(a_read, phase(s.b, s.g))
                if s.on(A_PREP):
                    pe.wait_ge(v_read, s.count(A_PREP) + 1)
                pe.matmul(m_ps[:, 3 * P:4 * P], x2_t[:, :], wf[:, :], start=True, stop=True).then_inc(d_full, 1)

            def last_output(half):
                if half == 0:
                    pe.wait_ge(s_read, STAGES * 2 * TILES)
                for t in (2 * half, 2 * half + 1):
                    pe.wait_ge(last_att_ready, t + 1)
                    pe.matmul(s_ps[:, t // 2, t % 2, tile(0)], last_att_n[:, tile(t)], wo[:, :], start=True, stop=True) \
                        .then_inc(last_wo_full, 1)

            pe.wait_ge(x_in_done, 16)
            for side, w in enumerate((wq, wk)):
                pe.wait_ge(w_in[side], 16)
                pe.matmul(s_ps[:, side, 0, :], w[:, :], x_in[:, :], start=True, stop=True).then_inc(first_full, 1)
                for half in range(2):
                    mm = pe.matmul(s_ps[64 * half:64 * half + 64, side, 1, :], w[:, 64 - 64 * half:128 - 64 * half],
                                   x_in[:, :], start=True, stop=True)
                mm.then_inc(first_full, 1)
            pe.wait_ge(w_in[2], 16)
            for t in range(TILES):
                mm = pe.matmul(t_ps[:, 0, tile(t)], x_in[:, tile(t)], wv[:, :], start=True, stop=True)
            mm.then_inc(first_v_full, 1)

            def stage(s):
                if isinstance(s.b, int) and s.count(A_SMAX) == 0:
                    pe.wait_ge(ident_done, 16)
                    pe.wait_ge(wf_wo_in, 2 * 16)
                    pe.wait_ge(setup_v, SETUP_V)
                    pe.wait_ge(setup_g, SETUP_G)
                for c in range(TILES):
                    for jj in range(2):
                        if s.on(0):
                            shifted_scores(s, c, 2 * jj)
                        if s.on(A_SMAX):
                            score_pair(s, c, jj)
                        if s.on(0):
                            shifted_scores(s, c, 2 * jj + 1)
                        if jj == 0:
                            if c == 0 and s.on(-1):
                                weighted_values(s, -1, TILES - 1)
                            if c > 0 and s.on(0):
                                weighted_values(s, 0, c - 1)
                    if c == 0 and s.on(A_WO):
                        phase_c(s)
                    if c == 1 and (s.on(A_FFN) or s.on(A_MROW)):
                        phase_a(s)
                    if c == 2 and s.on(A_PREP):
                        phase_b(s)
                    if c == 3 and s.on(A_FFN):
                        phase_d(s)
                if isinstance(s.b, int) and s.count(0) in LAST_DIVIDES:
                    last_output(LAST_DIVIDES.index(s.count(0)))

            run(stage, pe)

            for t in range(TILES):
                pe.wait_ge(last_out_ready, t + 1)
                pe.transpose(t_ps[:, t // 2, tile(t % 2)], last_x2[:, t, :], ident[:, :]).then_inc(last_x2_t_full, 1)
            for t in range(TILES):
                pe.wait_ge(last_x2_t_ready, t // 2 + 1)
                pe.matmul(s_ps[:, t // 2, t % 2, tile(1)], last_x2_t[:, tile(t)], wf[:, :], start=True, stop=True) \
                    .then_inc(last_ffn_full, 1)

        @block.scalar
        def _(act):
            act.wait_ge(first_v_full, 1)
            act.copy(v_nat[:, 0, :, :], t_ps[:, 0, :].rearrange("p (t d) -> p t d", d=D)).then_inc(v_read, TILES)

            def exp(s, c, j):
                k = GH * c + j
                if some(seen := s.count(0, GH * TILES, k + 1)):
                    act.wait_ge(t_full, seen)
                if j == 0:
                    if some(seen := s.count(-1, TILES, c + 1)):
                        act.wait_ge(pv_done, seen)
                act.activation(probs[:, c, j, :], t_ps[:, k % 2, :], ACT.Exp, scale=SCALE).then_inc(p_ready, 1)

            def phase_a_out(s):
                act.wait_ge(a_full, phase(s.b, s.g))
                if s.on(A_FFN):
                    last = act.copy(x2_t[:, :], m_ps[:, P:2 * P])
                if s.on(A_MROW):
                    n, uses = s.turn(A_MROW - 1)
                    if s.on(A_MROW - 1):
                        act.wait_ge(mrow_done[n], uses * 48)
                    last = act.copy(max_t[:, :], max_t_ps)
                last.then_inc(a_read, 1)

            def phase_b_out(s):
                n, uses = s.turn(A_PREP)
                act.wait_ge(b_full, s.count(A_PREP, 1, 1 - TILES))
                if s.on(A_PREP - 2) and not (isinstance(s.b, int) and s.count(A_PREP - 2) < TILES):
                    act.wait_ge(rope, s.count(A_PREP - 2, ROPE_STEPS, ROPE_STEPS))
                    m, uses = s.turn(A_PREP - 2)
                    act.wait_ge(swap_done[m], uses * 32)
                act.copy(qk_raw[:, n, :, :], m_ps[:, 0:2 * P].rearrange("p (a c) -> p a c", c=P)).then_inc(qk_read, 1)
                act.copy(v_nat[:, s.batch(A_PREP) & 3, s.slot(A_PREP), :], m_ps[:, 2 * P:3 * P]).then_inc(v_read, 1)

            def stage(s):
                for c in range(TILES):
                    for j in range(GH):
                        if s.on(0):
                            exp(s, c, j)
                        if c == 2 and j == 1 and (s.on(A_FFN) or s.on(A_MROW)):
                            phase_a_out(s)
                        if c == 3 and j == 1 and s.on(A_PREP):
                            phase_b_out(s)

            run(stage, act)

            for half in range(2):
                act.wait_ge(last_x2_t_full, 2 * half + 2)
                act.copy(last_x2_t[:, 2 * P * half:2 * P * half + 2 * P], t_ps[:, half, 0:2 * P]) \
                    .then_inc(last_x2_t_ready, 1)

        @block.vector
        def _(dve):
            def first_batch(side, step, half):
                c = slice(half * SEQ // 2, (half + 1) * SEQ // 2)
                part = lambda k: parts[:, 0, side, k, c]
                if step >= 2:
                    dve.wait_ge(first_rope, 2 * (side * FIRST_STEPS + step) + half - 1)
                if step == 0:
                    dve.wait_ge(first_full, 2 * side + 1)
                    op = dve.tensor_tensor(first_a[:, c], s_ps[:, side, 0, c], cos_sin[:, 0, c], ALU.mult)
                elif step == 1:
                    dve.wait_ge(first_full, 2 * side + 2)
                    op = dve.tensor_tensor(first_b[:, c], s_ps[:, side, 1, c], cos_sin[:, 1, c], ALU.mult)
                elif step == 2:
                    op = dve.tensor_tensor(first_r[:, c], first_a[:, c], first_b[:, c], ALU.add)
                elif step == 3:
                    op = dve.tensor_copy(part(0), first_r[:, c])
                elif step == 4:
                    op = dve.tensor_tensor(first_rest[:, c], first_r[:, c], part(0), ALU.subtract)
                elif step == 5:
                    op = dve.tensor_copy(part(1), first_rest[:, c])
                else:
                    op = dve.tensor_tensor(part(2), first_rest[:, c], part(1), ALU.subtract)
                op.then_inc(first_rope, 1)

            dve.wait_ge(table_in, 16)
            for side in range(2):
                for step in range(FIRST_STEPS):
                    for half in range(2):
                        first_batch(side, step, half)

            def signs():
                dve.wait_ge(wf_wo_in, 2 * 16)
                dve.tensor_scalar(wf_pos[:, :], wf_raw[:, :], 0.0, None, ALU.is_gt)
                dve.tensor_scalar(wf_neg[:, :], wf_raw[:, :], 0.0, None, ALU.is_lt).then_inc(setup_v, 1)
                dve.wait_ge(setup_v, 1)
                dve.tensor_tensor(wf[:, :], wf_pos[:, :], wf_neg[:, :], ALU.subtract).then_inc(setup_v, 1)

            def pair_max(s, k):
                c, jj = k // 2, k % 2
                if k == 0:
                    if some(seen := s.count(A_SMAX - 2, MSPLIT_STEPS, MSPLIT_STEPS)):
                        dve.wait_ge(msplit, seen)
                if some(seen := s.count(A_SMAX, 2 * TILES, k + 1)):
                    dve.wait_ge(s_full, seen)
                dve.tensor_reduce(neg_max[:, s.turn(A_SMAX)[0], 2 * jj:2 * jj + 2, c], s_ps[:, k % 2, :, :],
                                  AX.X, ALU.max, negate=True).then_inc(s_read, 1)

            def sums_out(s):
                if some(seen := s.count(-1, TILES, TILES)):
                    dve.wait_ge(pv_done, seen)
                if s.on(-2):
                    n, uses = s.turn(-2)
                    dve.wait_ge(o_out_done[n], uses * 16)
                dve.tensor_copy(o_sum[:, :], o_ps[:, :]).then_inc(o_read, 1)

            def add_first(s, ahead):
                dve.wait_ge(c_full, s.count(ahead) + 1)
                dve.wait_ge(x_res_done, (s.batch(ahead) + 1) * 16)
                if some(seen := s.count(ahead - 1) + 1):
                    dve.wait_ge(x2_ready, seen)
                dve.tensor_tensor(z1[:, :], m_ps[:, 0:P], x_res[:, s.slot(ahead), :], ALU.add).then_inc(z1_ready, 1)

            def add_second(s, ahead):
                n, uses = s.turn(ahead)
                dve.wait_ge(d_full, s.count(ahead) + 1)
                if some(seen := s.count(ahead - 1) + 1):
                    dve.wait_ge(y_ready, seen)
                dve.tensor_tensor(z2[:, :], m_ps[:, 3 * P:4 * P], x2[:, n, :], ALU.add).then_inc(z2_ready, 1)

            def stats(s, ahead, z, st, ready, done):
                dve.wait_ge(ready, s.count(ahead) + 1)
                dve.bn_stats(st[:, :], z[:, :]).then_inc(done, 1)

            def moments(s, ahead, st, mv, ready, done):
                dve.wait_ge(ready, s.count(ahead) + 1)
                dve.sem_inc(waited_v, 1)
                dve.bn_aggr(mv[:, :], st[:, :]).then_inc(done, 1)

            def factors(s, ahead, mv, nr, ready, done):
                dve.wait_ge(ready, s.count(ahead) + 1)
                dve.tensor_scalar(nr[:, 0:1], mv[:, 0:1], -1.0, None, ALU.mult)
                dve.tensor_scalar(nr[:, 1:2], mv[:, 1:2], EPS, None, ALU.add).then_inc(done, 1)

            def reciprocals(s):
                b2 = s.batch(A_RCP)
                dve.wait_ge(den_in_done, (b2 + 1) * 16)
                if some(seen := b2 * 16):
                    dve.wait_ge(rcp_out_done, seen)
                dve.reciprocal(den_rcp[:, :], den[:, :]).then_inc(rcp_ready, 1)

            def last_reciprocals(half):
                if half == 0:
                    dve.wait_ge(last_in_done[1], GH * 16)
                for t in (2 * half, 2 * half + 1):
                    dve.reciprocal(last_att[:, 1, tile(t)], last_att[:, 1, tile(t)]).then_inc(last_rcp_ready, 1)

            def stage(s):
                if isinstance(s.b, int) and s.count(0) in LAST_DIVIDES:
                    last_reciprocals(LAST_DIVIDES.index(s.count(0)))
                if isinstance(s.b, int) and s.count(A_ROPE) == TILES:
                    signs()
                if s.on(A_LN2):
                    add_second(s, A_LN2)
                for k in range(2 * TILES):
                    if s.on(A_SMAX):
                        pair_max(s, k)
                    if k == 0 and s.on(-1):
                        sums_out(s)
                    if k == 0 and s.on(A_RCP) and s.slot(A_RCP) == 0:
                        reciprocals(s)
                    if k == 1 and s.on(A_LN2):
                        stats(s, A_LN2, z2, st2, z2_ready, st2_ready)
                    if k == 1 and s.on(A_WO):
                        add_first(s, A_WO)
                    if k == 2 and s.on(A_LN2):
                        moments(s, A_LN2, st2, mv2, st2_ready, mv2_ready)
                    if k == 3 and s.on(A_LN2):
                        factors(s, A_LN2, mv2, nr2, mv2_ready, ln2_ready)
                    if k == 3 and s.on(A_WO):
                        stats(s, A_WO, z1, st1, z1_ready, st1_ready)
                    if k == 4 and s.on(A_WO):
                        moments(s, A_WO, st1, mv1, st1_ready, mv1_ready)
                        factors(s, A_WO, mv1, nr1, mv1_ready, ln1_ready)

            run(stage, dve)

            def last_add(layer, t):
                full, add = ((last_wo_full, last_x), (last_ffn_full, last_x2))[layer]
                dve.wait_ge(full, t + 1)
                dve.tensor_tensor(last_z[:, t, :], s_ps[:, t // 2, t % 2, tile(layer)], add[:, t, :], ALU.add) \
                    .then_inc(last_z_ready, 1)

            def last_stats(layer, t):
                dve.wait_ge(last_z_ready, TILES * layer + t + 1)
                dve.bn_stats(last_st[:, t, :], last_z[:, t, :]).then_inc(last_st_ready, 1)

            def last_moments(layer, half):
                first = 2 * half
                for t in (first, first + 1):
                    dve.wait_ge(last_st_ready, TILES * layer + t + 1)
                    dve.bn_aggr(last_mv[:, t, :], last_st[:, t, :]).then_inc(last_mv_ready, 1)
                dve.wait_ge(last_mv_ready, TILES * layer + first + 2)
                dve.tensor_scalar(last_nr[:, 0, first:first + 2], last_mv[:, first:first + 2, 0], -1.0, None, ALU.mult)
                dve.tensor_scalar(last_nr[:, 1, first:first + 2], last_mv[:, first:first + 2, 1], EPS, None, ALU.add) \
                    .then_inc(last_nr_ready, 1)

            def last_normalise(layer, half, out):
                dve.wait_ge(last_nr_ready, 2 * layer + half + 1)
                dve.wait_ge(last_rstd_ready, 2 * layer + half + 1)
                for t in (2 * half, 2 * half + 1):
                    dve.tensor_scalar(out[:, t, :], last_z[:, t, :], last_nr[:, 0, t:t + 1], last_rstd[:, t:t + 1],
                                      ALU.add, ALU.mult).then_inc(last_out_ready, 1)

            dve.wait_ge(last_x_done, 16)
            for layer, out in ((0, last_x2), (1, y)):
                for half in range(2):
                    for t in (2 * half, 2 * half + 1):
                        last_add(layer, t)
                        last_stats(layer, t)
                    last_moments(layer, half)
                if layer == 1:
                    dve.wait_ge(y_out_done, (BATCH - 1) * 16)
                for half in range(2):
                    last_normalise(layer, half, out)

        @block.gpsimd
        def _(pool):
            ones2 = float(np.array([0x3F803F80], np.uint32).view(np.float32)[0])
            pool.memset(k_slot[:, :, :, :].bitcast(fp32), 0.0).then_inc(setup_g, 1)
            pool.memset(q_slot[:, :, :, :].bitcast(fp32), 0.0).then_inc(setup_g, 1)
            pool.wait_ge(setup_g, 2)
            pool.memset(k_slot[MAX_ROW:QK_ROWS, :, :, :].bitcast(fp32), ones2).then_inc(setup_g, 1)
            pool.wait_ge(setup_g, 3)
            pool.memset(minus_half[:, :], -0.5).then_inc(setup_g, 1)
            pool.memset(v_slot[:, :, :, :, HD:HD + 1], 1.0).then_inc(setup_g, 1)
            pool.memset(v_slot[:, :, :, :, HD + 1:32], 0.0).then_inc(setup_g, 1)
            pool.wait_ge(setup_g, 6)
            pool.wait_ge(ident_done, 16)
            pool.tensor_copy(ident_b[:, :], ident[:, :]).then_inc(setup_g, 1)
            pool.wait_ge(table_in, 16)

            def split_maxima(s):
                n, _ = s.turn(A_MROW)
                m = neg_max[:, n, :, :].rearrange("p j t -> p (j t)")
                at = lambda k: s.count(A_MROW, MSPLIT_STEPS, k)
                if some(seen := s.count(A_MROW, 2 * TILES, 2 * TILES)):
                    pool.wait_ge(s_read, seen)
                    pool.sem_inc(waited_g, 1)
                if some(seen := phase(s.b, s.g) - 1):
                    pool.wait_ge(a_full, seen)
                    pool.sem_inc(waited_g, 1)
                pool.tensor_copy(max_parts[:, 0, :], m).then_inc(msplit, 1)
                if some(seen := at(1)):
                    pool.wait_ge(msplit, seen)
                    pool.sem_inc(waited_g, 1)
                pool.tensor_tensor(max_rest[:, :], m, max_parts[:, 0, :], ALU.subtract).then_inc(msplit, 1)
                if some(seen := at(2)):
                    pool.wait_ge(msplit, seen)
                    pool.sem_inc(waited_g, 1)
                pool.tensor_copy(max_parts[:, 1, :], max_rest[:, :]).then_inc(msplit, 1)
                if some(seen := at(3)):
                    pool.wait_ge(msplit, seen)
                    pool.sem_inc(waited_g, 1)
                pool.tensor_tensor(max_parts[:, 2, :], max_rest[:, :], max_parts[:, 1, :], ALU.subtract).then_inc(msplit, 1)

            def rotate(s):
                n, uses = s.turn(A_ROPE)
                t = s.slot(A_ROPE)
                tab = lambda k: cos_sin[:, k:k + 1, P * t:P * t + P].to_broadcast([P, 2, P])
                at = lambda k: s.count(A_ROPE, ROPE_STEPS, k)
                pool.wait_ge(qk_read, s.count(A_ROPE) + 1)
                pool.sem_inc(waited_g, 1)
                pool.tensor_tensor(rope_a[:, :, :], qk_raw[:, n, :, :], tab(0), ALU.mult).then_inc(rope, 1)
                pool.wait_ge(swap_done[n], uses * 32)
                pool.sem_inc(waited_g, 1)
                pool.tensor_tensor(rope_b[:, :, :], qk_swap[:, n, :, :], tab(1), ALU.mult).then_inc(rope, 1)
                if some(seen := at(2)):
                    pool.wait_ge(rope, seen)
                    pool.sem_inc(waited_g, 1)
                pool.tensor_tensor(rope_r[:, :, :], rope_a[:, :, :], rope_b[:, :, :], ALU.add).then_inc(rope, 1)

            def split_rotated(s):
                t = s.slot(A_ROPE)
                b2 = s.batch(A_ROPE)
                part = lambda k: parts[:, b2 & 1, :, k, P * t:P * t + P]
                at = lambda k: s.count(A_ROPE, ROPE_STEPS, k)
                if t == 0:
                    if some(seen := (b2 - 1) * SPREAD):
                        pool.wait_ge(spread_done, seen)
                        pool.sem_inc(waited_g, 1)
                if some(seen := at(3)):
                    pool.wait_ge(rope, seen)
                    pool.sem_inc(waited_g, 1)
                pool.tensor_copy(part(0), rope_r[:, :, :]).then_inc(rope, 1)
                if some(seen := at(4)):
                    pool.wait_ge(rope, seen)
                    pool.sem_inc(waited_g, 1)
                pool.tensor_tensor(rope_rest[:, :, :], rope_r[:, :, :], part(0), ALU.subtract).then_inc(rope, 1)
                if some(seen := at(5)):
                    pool.wait_ge(rope, seen)
                    pool.sem_inc(waited_g, 1)
                pool.tensor_copy(part(1), rope_rest[:, :, :]).then_inc(rope, 1)
                if some(seen := at(6)):
                    pool.wait_ge(rope, seen)
                    pool.sem_inc(waited_g, 1)
                pool.tensor_tensor(part(2), rope_rest[:, :, :], part(1), ALU.subtract).then_inc(rope, 1)

            def stage_values(s):
                g = s.slot(A_MROW)
                b2 = s.batch(A_MROW)
                pool.wait_ge(v_read, (b2 + 1) * TILES)
                pool.sem_inc(waited_g, 1)
                if some(seen := s.count(A_MROW - GROUPS, TILES, TILES)):
                    pool.wait_ge(pv_done, seen)
                    pool.sem_inc(waited_g, 1)
                pool.tensor_copy(v_slot[:, g, :, :, 0:HD],
                                 v_nat[:, b2 & 3, :, 32 * g:32 * g + 32].rearrange("p t (j d) -> p t j d", d=HD)) \
                    .then_inc(v_staged, 1)

            def normalise(s, ahead, z, nr, rstd, out, ready, powered, done):
                pool.wait_ge(ready, s.count(ahead) + 1)
                pool.sem_inc(waited_g, 1)
                pool.tensor_tensor(rstd[:, :], nr[:, 1:2], minus_half[:, 0:1], ALU.pow).then_inc(powered, 1)
                pool.wait_ge(powered, s.count(ahead) + 1)
                pool.sem_inc(waited_g, 1)
                pool.tensor_scalar(out, z[:, :], nr[:, 0:1], rstd[:, :], ALU.add, ALU.mult).then_inc(done, 1)

            def divide(s, ahead):
                t = s.slot(ahead)
                pool.wait_ge(att_in_done, (s.batch(ahead) + 1) * ((GH + 1) * 16))
                pool.sem_inc(waited_g, 1)
                if some(seen := s.count(ahead - 1)):
                    pool.wait_ge(c_full, seen)
                    pool.sem_inc(waited_g, 1)
                pool.tensor_tensor(att_n[:, s.turn(ahead)[0], :], att[:, 0, tile(t)], att[:, 1, tile(t)], ALU.mult) \
                    .then_inc(att_ready, 1)

            def last_divide(half):
                if half == 0:
                    pool.wait_ge(last_in_done[0], 16)
                for t in (2 * half, 2 * half + 1):
                    pool.wait_ge(last_rcp_ready, t + 1)
                    pool.tensor_tensor(last_att_n[:, tile(t)], last_att[:, 0, tile(t)], last_att[:, 1, tile(t)],
                                       ALU.mult).then_inc(last_att_ready, 1)

            def stage(s):
                if isinstance(s.b, int) and s.count(0) in LAST_DIVIDES:
                    last_divide(LAST_DIVIDES.index(s.count(0)))
                if s.on(A_MROW):
                    split_maxima(s)
                if s.on(A_DIVIDE):
                    divide(s, A_DIVIDE)
                if s.on(A_ROPE):
                    rotate(s)
                    split_rotated(s)
                if s.on(A_LN2):
                    if s.slot(A_LN2) == 0:
                        if some(seen := s.batch(A_LN2) * 16):
                            pool.wait_ge(y_out_done, seen)
                            pool.sem_inc(waited_g, 1)
                    normalise(s, A_LN2, z2, nr2, rstd2, y[:, s.slot(A_LN2), :], ln2_ready, pow2_ready, y_ready)
                if s.on(A_MROW):
                    stage_values(s)
                if s.on(A_WO):
                    if some(seen := s.count(A_WO - 2) + 1):
                        pool.wait_ge(z2_ready, seen)
                        pool.sem_inc(waited_g, 1)
                    normalise(s, A_WO, z1, nr1, rstd1, x2[:, s.turn(A_WO)[0], :], ln1_ready, pow1_ready, x2_ready)

            run(stage, pool)

            for layer in range(2):
                for half in range(2):
                    ts = slice(2 * half, 2 * half + 2)
                    pool.wait_ge(last_nr_ready, 2 * layer + half + 1)
                    pool.tensor_tensor(last_rstd[:, ts], last_nr[:, 1, ts], minus_half[:, ts], ALU.pow) \
                        .then_inc(last_rstd_ready, 1)


def rope_table():
    import numpy as np
    inv = (np.float32(1.0) / np.power(np.float32(10000.0), np.arange(0, HD, 2, dtype=np.float32) / np.float32(HD))).astype(np.float32)
    ang = (np.arange(SEQ, dtype=np.float32)[None, :] * inv[:, None]).astype(np.float32)
    cos, sin = np.cos(ang).astype(np.float32), np.sin(ang).astype(np.float32)
    tab = np.zeros((2, HD // 2, HEADS, 2, SEQ), np.float32)
    tab[:, :, :, 0, :] = cos[None, :, None, :]
    tab[0, :, :, 1, :] = -sin[:, None, :]
    tab[1, :, :, 1, :] = sin[:, None, :]
    return tab.reshape(P, 2, SEQ)


def kernel(**inputs):
    import numpy as np
    import concourse.bacc as bacc
    from concourse.bass_utils import run_bass_kernel_spmd

    def rows_of_qk(w):
        w = w.reshape(GROUPS, GH, HD // 2, 2, D).transpose(3, 2, 1, 0, 4).reshape(D, D)
        return np.ascontiguousarray(w.T)

    a = {k: np.asarray(v) for k, v in inputs.items()}
    wo_rows = a["L0_attn_wo"].T.reshape(GROUPS, GH, HD, D).transpose(1, 2, 0, 3).reshape(D, D)
    arrays = {
        "x": np.ascontiguousarray(a["L0_attn_x"]),
        "x_t": np.ascontiguousarray(a["L0_attn_x"].transpose(0, 2, 1)),
        "wq_t": rows_of_qk(a["L0_attn_wq"]),
        "wk_t": rows_of_qk(a["L0_attn_wk"]),
        "wv_t": np.ascontiguousarray(a["L0_attn_wv"].T),
        "wo_t": np.ascontiguousarray(wo_rows),
        "wf_t": np.ascontiguousarray(a["L0_ffn_weight"].T),
        "rope_tab": rope_table(),
        "ident_in": np.eye(P, dtype=np.float32),
    }
    nc = bacc.Bacc("TRN2", target_bir_lowering=False, num_devices=1)
    args = [nc.dram_tensor(k, v.shape, mybir.dt.from_np(v.dtype), kind="ExternalInput").ap() for k, v in arrays.items()]
    out = nc.dram_tensor("y_out", (BATCH, SEQ, D), mybir.dt.float32, kind="ExternalOutput").ap()
    body(nc, *args, out)
    r = run_bass_kernel_spmd(nc, [arrays], core_ids=[0])
    return r.results[0]["y_out"]
```
